# Optimizing a Trainium2 kernel written in Bass

```python
import numpy as np
import jax
import jax.numpy as jnp

def _softmax(x, axis=-1):
    return jax.nn.softmax(x, axis=axis)

def _gelu(x):
    return jax.nn.gelu(x, approximate=True)

def _silu(x):
    return jax.nn.silu(x)

def _sigmoid(x):
    return jax.nn.sigmoid(x)

def _layernorm(x, axis=-1, eps=1e-05):
    m = jnp.mean(x, axis=axis, keepdims=True)
    v = jnp.var(x, axis=axis, keepdims=True)
    return (x - m) / jnp.sqrt(v + eps)

def _scatter_add(tgt, idx, src, axis=0):
    return tgt.at[idx].add(src)

def _segment_sum(src, seg, n):
    return jax.ops.segment_sum(src, seg, n)
kernel_name = 'mk_macaron_d2_jaxref_r8_0ed636'

def setup_inputs(seed: int=0):
    np.random.seed(seed)
    _w = jnp.asarray

    def _L0_attn_setup():
        import jax, jax.numpy as jnp
        import numpy as np
        B, L, D, S = (4, 256, 128, 16)
        key = jax.random.key(seed)
        ks = jax.random.split(key, 8)
        inv_d = 1.0 / np.sqrt(D)
        inv_s = 1.0 / np.sqrt(S)
        A_log = jnp.broadcast_to(jnp.clip(jnp.log(jnp.arange(1, S + 1, dtype=jnp.float32)), -7.0, None), (D, S))
        return {'x': jax.random.normal(ks[0], (B, L, D), jnp.float32), 'A_log': A_log, 'W_B': jax.random.uniform(ks[1], (S, D), jnp.float32, -inv_d, inv_d), 'W_C': jax.random.uniform(ks[2], (D, S), jnp.float32, -inv_s, inv_s), 'D_skip': jnp.ones((D,), jnp.float32), 'log_dt': jax.random.normal(ks[3], (D,), jnp.float32) * 0.01 - 4.0, 'W_in': jax.random.uniform(ks[4], (2 * D, D), jnp.float32, -inv_d, inv_d), 'b_in': jax.random.uniform(ks[5], (2 * D,), jnp.float32, -inv_d, inv_d), 'W_out': jax.random.uniform(ks[6], (D, D), jnp.float32, -inv_d, inv_d), 'b_out': jax.random.uniform(ks[7], (D,), jnp.float32, -inv_d, inv_d), 'ln_g': jnp.ones((D,), jnp.float32), 'ln_b': jnp.zeros((D,), jnp.float32)}
    _L0_attn_in = _L0_attn_setup()

    def _L0_ffn_setup():
        import jax, jax.numpy as jnp
        import numpy as np
        B, S, H, E = (4, 256, 128, 8)
        key = jax.random.key(seed)
        k1, k2, k3 = jax.random.split(key, 3)
        scale_w = 1.0 / np.sqrt(H)
        return {'x': jax.random.normal(k1, (B, S, H), dtype=jnp.float32), 'router_w': jax.random.normal(k2, (H, E), dtype=jnp.float32) * scale_w, 'router_b': jnp.zeros((E,), dtype=jnp.float32), 'expert_w': jax.random.normal(k3, (E, H, H), dtype=jnp.float32) * scale_w, 'expert_b': jnp.zeros((E, H), dtype=jnp.float32)}
    _L0_ffn_in = _L0_ffn_setup()

    def _L1_attn_setup():
        import jax, jax.numpy as jnp
        import numpy as np
        import math
        D_MODEL = 128
        NUM_HEADS = 16
        D_K = D_MODEL // NUM_HEADS
        THETA = 10000.0
        BATCH = 2
        SEQ = 256

        def _trunc_normal(key, shape, std):
            return jax.random.truncated_normal(key, -3.0, 3.0, shape, jnp.float32) * std

        def _apply_rope(t):
            S = t.shape[-2]
            inv_freq = 1.0 / THETA ** (jnp.arange(0, D_K, 2, dtype=jnp.float32) / D_K)
            ang = jnp.arange(S, dtype=jnp.float32)[:, None] * inv_freq[None, :]
            cos, sin = (jnp.cos(ang), jnp.sin(ang))
            t1 = t[..., ::2]
            t2 = t[..., 1::2]
            r1 = t1 * cos - t2 * sin
            r2 = t1 * sin + t2 * cos
            out = jnp.stack([r1, r2], axis=-1).reshape(t.shape)
            return out
        key = jax.random.key(seed)
        kx, kq, kk, kv, ko = jax.random.split(key, 5)
        std = math.sqrt(2.0 / (D_MODEL + D_MODEL))
        return {'x': jax.random.normal(kx, (BATCH, SEQ, D_MODEL), jnp.float32), 'Wq': _trunc_normal(kq, (D_MODEL, D_MODEL), std), 'Wk': _trunc_normal(kk, (D_MODEL, D_MODEL), std), 'Wv': _trunc_normal(kv, (D_MODEL, D_MODEL), std), 'Wo': _trunc_normal(ko, (D_MODEL, D_MODEL), std)}
    _L1_attn_in = _L1_attn_setup()

    def _L1_ffn_setup():
        import jax, jax.numpy as jnp
        import numpy as np
        D_IN, D_HID = (128, 512)

        def _ternary(key, shape):
            return jax.random.randint(key, shape, -1, 2).astype(jnp.float32)

        def _tlin(x, w, s):
            return jnp.einsum('bsi,oi->bso', x, w) * s
        key = jax.random.key(seed)
        ks = jax.random.split(key, 12)
        inv = lambda fan: 1.0 / np.sqrt(fan).astype(np.float32)
        return {'x': jax.random.normal(ks[0], (4, 256, D_IN), dtype=jnp.float32), 'w1_w': _ternary(ks[1], (D_HID, D_IN)), 'w1_s': jax.random.uniform(ks[2], (D_HID,), dtype=jnp.float32) * inv(D_IN), 'w2_w': _ternary(ks[3], (D_HID, D_IN)), 'w2_s': jax.random.uniform(ks[4], (D_HID,), dtype=jnp.float32) * inv(D_IN), 'h1_w': _ternary(ks[5], (D_HID, D_HID)), 'h1_s': jax.random.uniform(ks[6], (D_HID,), dtype=jnp.float32) * inv(D_HID), 'h2_w': _ternary(ks[7], (D_HID, D_HID)), 'h2_s': jax.random.uniform(ks[8], (D_HID,), dtype=jnp.float32) * inv(D_HID), 'w3_w': _ternary(ks[9], (D_IN, D_HID)), 'w3_s': jax.random.uniform(ks[10], (D_IN,), dtype=jnp.float32) * inv(D_HID)}
    _L1_ffn_in = _L1_ffn_setup()
    _d = {'L0_attn_x': _L0_attn_in['x'], 'L0_attn_A_log': _L0_attn_in['A_log'], 'L0_attn_W_B': _L0_attn_in['W_B'], 'L0_attn_W_C': _L0_attn_in['W_C'], 'L0_attn_D_skip': _L0_attn_in['D_skip'], 'L0_attn_log_dt': _L0_attn_in['log_dt'], 'L0_attn_W_in': _L0_attn_in['W_in'], 'L0_attn_b_in': _L0_attn_in['b_in'], 'L0_attn_W_out': _L0_attn_in['W_out'], 'L0_attn_b_out': _L0_attn_in['b_out'], 'L0_attn_ln_g': _L0_attn_in['ln_g'], 'L0_attn_ln_b': _L0_attn_in['ln_b'], 'L0_ffn_router_w': _L0_ffn_in['router_w'], 'L0_ffn_router_b': _L0_ffn_in['router_b'], 'L0_ffn_expert_w': _L0_ffn_in['expert_w'], 'L0_ffn_expert_b': _L0_ffn_in['expert_b'], 'L1_attn_Wq': _L1_attn_in['Wq'], 'L1_attn_Wk': _L1_attn_in['Wk'], 'L1_attn_Wv': _L1_attn_in['Wv'], 'L1_attn_Wo': _L1_attn_in['Wo'], 'L1_ffn_w1_w': _L1_ffn_in['w1_w'], 'L1_ffn_w1_s': _L1_ffn_in['w1_s'], 'L1_ffn_w2_w': _L1_ffn_in['w2_w'], 'L1_ffn_w2_s': _L1_ffn_in['w2_s'], 'L1_ffn_h1_w': _L1_ffn_in['h1_w'], 'L1_ffn_h1_s': _L1_ffn_in['h1_s'], 'L1_ffn_h2_w': _L1_ffn_in['h2_w'], 'L1_ffn_h2_s': _L1_ffn_in['h2_s'], 'L1_ffn_w3_w': _L1_ffn_in['w3_w'], 'L1_ffn_w3_s': _L1_ffn_in['w3_s']}
    _x0 = _d['L0_attn_x']
    _d['L0_attn_x'] = jax.random.normal(jax.random.fold_in(jax.random.key(seed), 1), (1, 2048, 128), dtype=_x0.dtype)
    del _x0
    return _d

def reference(L0_attn_x, L0_attn_A_log, L0_attn_W_B, L0_attn_W_C, L0_attn_D_skip, L0_attn_log_dt, L0_attn_W_in, L0_attn_b_in, L0_attn_W_out, L0_attn_b_out, L0_attn_ln_g, L0_attn_ln_b, L0_ffn_router_w, L0_ffn_router_b, L0_ffn_expert_w, L0_ffn_expert_b, L1_attn_Wq, L1_attn_Wk, L1_attn_Wv, L1_attn_Wo, L1_ffn_w1_w, L1_ffn_w1_s, L1_ffn_w2_w, L1_ffn_w2_s, L1_ffn_h1_w, L1_ffn_h1_s, L1_ffn_h2_w, L1_ffn_h2_s, L1_ffn_w3_w, L1_ffn_w3_s):

    def _L0_attn_ref(x, A_log, W_B, W_C, D_skip, log_dt, W_in, b_in, W_out, b_out, ln_g, ln_b):
        import jax, jax.numpy as jnp
        import numpy as np
        B, L, D, S = (4, 256, 128, 16)
        Bb, Ll, Dd = x.shape
        residual = x
        mu = x.mean(-1, keepdims=True)
        var = ((x - mu) ** 2).mean(-1, keepdims=True)
        xn = (x - mu) / jnp.sqrt(var + 1e-05) * ln_g + ln_b
        xz = xn @ W_in.T + b_in
        x_proj, z = jnp.split(xz, 2, axis=-1)
        z = jax.nn.silu(z)
        dt = jnp.clip(jnp.exp(log_dt), 0.0001, 1.0)
        A_bar = jnp.exp(-jnp.exp(A_log) * dt[:, None])
        A_bar = jnp.clip(A_bar, 1e-08, 1.0 - 1e-08)
        B_proj = x_proj @ W_B.T * dt.mean()
        t_idx = jnp.arange(Ll, dtype=jnp.float32)
        log_A = jnp.log(A_bar)
        A_mean = jnp.exp(t_idx[:, None, None] * log_A[None]).mean(axis=1)
        kernel = jnp.flip(A_mean.T, -1)[:, None, :]
        lhs = jnp.transpose(B_proj, (0, 2, 1))
        x_mean = jax.lax.conv_general_dilated(lhs, kernel, window_strides=(1,), padding=((Ll - 1, 0),), dimension_numbers=('NCH', 'OIH', 'NCH'), feature_group_count=kernel.shape[0])
        x_mean = jnp.transpose(x_mean, (0, 2, 1))
        y = x_mean @ W_C.T + D_skip * x_proj
        y = y * z
        y = y @ W_out.T + b_out
        return y + residual

    def _L0_ffn_ref(x, router_w, router_b, expert_w, expert_b):
        import jax, jax.numpy as jnp
        import numpy as np
        B, S, H, E = (4, 256, 128, 8)
        b, s, h = x.shape
        xt = x.reshape(b * s, h)
        logits = xt @ router_w + router_b
        probs = jax.nn.softmax(logits, axis=-1)
        gate = jnp.max(probs, axis=-1)
        idx = jnp.argmax(probs, axis=-1)
        out_all = jnp.einsum('th,ehd->ted', xt, expert_w) + expert_b[None, :, :]
        e_out = jnp.take_along_axis(out_all, idx[:, None, None], axis=1)[:, 0, :]
        y = gate[:, None] * e_out
        return y.reshape(b, s, h)

    def _L1_attn_ref(x, Wq, Wk, Wv, Wo):
        import jax, jax.numpy as jnp
        import numpy as np
        import math
        D_MODEL = 128
        NUM_HEADS = 16
        D_K = D_MODEL // NUM_HEADS
        THETA = 10000.0
        BATCH = 2
        SEQ = 256

        def _trunc_normal(key, shape, std):
            return jax.random.truncated_normal(key, -3.0, 3.0, shape, jnp.float32) * std

        def _apply_rope(t):
            S = t.shape[-2]
            inv_freq = 1.0 / THETA ** (jnp.arange(0, D_K, 2, dtype=jnp.float32) / D_K)
            ang = jnp.arange(S, dtype=jnp.float32)[:, None] * inv_freq[None, :]
            cos, sin = (jnp.cos(ang), jnp.sin(ang))
            t1 = t[..., ::2]
            t2 = t[..., 1::2]
            r1 = t1 * cos - t2 * sin
            r2 = t1 * sin + t2 * cos
            out = jnp.stack([r1, r2], axis=-1).reshape(t.shape)
            return out
        B, S, _ = x.shape

        def proj(W):
            return (x @ W.T).reshape(B, S, NUM_HEADS, D_K).transpose(0, 2, 1, 3)
        q = _apply_rope(proj(Wq))
        k = _apply_rope(proj(Wk))
        v = proj(Wv)
        scores = jnp.einsum('bhqd,bhkd->bhqk', q, k) / math.sqrt(D_K)
        causal = jnp.tril(jnp.ones((S, S), dtype=bool))
        scores = jnp.where(causal, scores, -jnp.inf)
        attn = jax.nn.softmax(scores, axis=-1)
        ctx = jnp.einsum('bhqk,bhkd->bhqd', attn, v)
        ctx = ctx.transpose(0, 2, 1, 3).reshape(B, S, D_MODEL)
        return ctx @ Wo.T

    def _L1_ffn_ref(x, w1_w, w1_s, w2_w, w2_s, h1_w, h1_s, h2_w, h2_s, w3_w, w3_s):
        import jax, jax.numpy as jnp
        import numpy as np
        D_IN, D_HID = (128, 512)

        def _ternary(key, shape):
            return jax.random.randint(key, shape, -1, 2).astype(jnp.float32)

        def _tlin(x, w, s):
            return jnp.einsum('bsi,oi->bso', x, w) * s
        h = jax.nn.silu(_tlin(x, w1_w, w1_s)) * _tlin(x, w2_w, w2_s)
        h = jax.nn.gelu(_tlin(h, h1_w, h1_s), approximate=False)
        h = jax.nn.gelu(_tlin(h, h2_w, h2_s), approximate=False)
        return _tlin(h, w3_w, w3_s)
    x = L0_attn_x
    x = x + 0.5 * _L0_ffn_ref(_layernorm(x, axis=-1), L0_ffn_router_w, L0_ffn_router_b, L0_ffn_expert_w, L0_ffn_expert_b)
    x = x + _L0_attn_ref(_layernorm(x, axis=-1), L0_attn_A_log, L0_attn_W_B, L0_attn_W_C, L0_attn_D_skip, L0_attn_log_dt, L0_attn_W_in, L0_attn_b_in, L0_attn_W_out, L0_attn_b_out, L0_attn_ln_g, L0_attn_ln_b)
    x = x + 0.5 * _L0_ffn_ref(_layernorm(x, axis=-1), L0_ffn_router_w, L0_ffn_router_b, L0_ffn_expert_w, L0_ffn_expert_b)
    x = x + 0.5 * _L1_ffn_ref(_layernorm(x, axis=-1), L1_ffn_w1_w, L1_ffn_w1_s, L1_ffn_w2_w, L1_ffn_w2_s, L1_ffn_h1_w, L1_ffn_h1_s, L1_ffn_h2_w, L1_ffn_h2_s, L1_ffn_w3_w, L1_ffn_w3_s)
    x = x + _L1_attn_ref(_layernorm(x, axis=-1), L1_attn_Wq, L1_attn_Wk, L1_attn_Wv, L1_attn_Wo)
    x = x + 0.5 * _L1_ffn_ref(_layernorm(x, axis=-1), L1_ffn_w1_w, L1_ffn_w1_s, L1_ffn_w2_w, L1_ffn_w2_s, L1_ffn_h1_w, L1_ffn_h1_s, L1_ffn_h2_w, L1_ffn_h2_s, L1_ffn_w3_w, L1_ffn_w3_s)
    return x

_drawn_inputs = setup_inputs


def setup_inputs(seed=0):
    import zlib

    import numpy as np

    out = dict(_drawn_inputs(seed))
    spreads = {'L0_attn_D_skip': (1.0, 0.2),
     'L0_attn_ln_g': (1.0, 0.2),
     'L0_attn_ln_b': (0.0, 0.1),
     'L0_ffn_router_b': (0.0, 0.1),
     'L0_ffn_expert_b': (0.0, 0.1)}
    factors = {}
    for name, (base, spread) in spreads.items():
        noise = np.random.default_rng([zlib.crc32(name.encode()), seed]).standard_normal(out[name].shape)
        drawn = base * np.exp(spread * noise) if base else spread * noise
        out[name] = jnp.asarray(drawn.astype(out[name].dtype))
    for name, factor in factors.items():
        out[name] = (out[name] * factor).astype(out[name].dtype)
    return out
```

```python
import math
from contextlib import ExitStack

import numpy as np

import concourse.bass as bass
from concourse import mybir

F32 = mybir.dt.float32
F32R = mybir.dt.float32r
BF16 = mybir.dt.bfloat16
I32 = mybir.dt.int32
ALU = mybir.AluOpType
ACT = mybir.ActivationFunctionType
AX = mybir.AxisListType

P = 128
T = 2048
D = 128
NT = T // P
CH = 512
NC = T // CH
TPC = CH // P
E = 8
S = 16
HID = 512
HB = HID // P
NH = 16
DK = D // NH
G = 4
EPS = 1e-5
NEG = -1e30
SCALE = 1.0 / math.sqrt(DK)
PARTS = 3
PAIRS = [(a, b) for a in range(PARTS) for b in range(PARTS)]
KR = len(PAIRS) * DK
MR = 2

COL = {}
for _name, _n in (("ln_g", 1), ("ln_b", 1), ("b_x", 1), ("b_z", 1), ("D_skip", 1), ("log_dt", 1),
                  ("w1_s", HB), ("w2_s", HB), ("h1_s", HB), ("h2_s", HB), ("A_log", S)):
    COL[_name] = (sum(n for _, n in COL.values()), _n)
NCOL = sum(n for _, n in COL.values())
ROW = {}
for _name, _n in (("router_b", E), ("expert_b", E * D), ("b_out", D), ("log_dt", D), ("A_log", S * D), ("w3_s", D)):
    ROW[_name] = (sum(n for _, n in ROW.values()), _n)
NROW = sum(n for _, n in ROW.values())


class Mark:

    def __init__(self, owner):
        self.owner, self.used, self.value = owner, False, None


class Dmas:

    def __init__(self, sem):
        self.sem, self.n = sem, 0
        self.mark = Mark(self)


class Banks:

    def __init__(self, ids, readers):
        self.ids, self.readers, self.at = ids, readers, 0

    def take(self):
        b = self.ids[self.at % len(self.ids)]
        self.at += 1
        return b, list(self.readers[b])

    def give(self, b, *marks):
        self.readers[b] = list(marks)


def build(nc, dram, out):
    ctx = ExitStack()
    with ctx:
        queues = {n: [] for n in ("tensor", "vector", "scalar", "gpsimd", "sync")}
        sems = {n: ctx.enter_context(nc.semaphore(f"done_{n}")) for n in ("tensor", "vector", "scalar", "gpsimd")}

        def put(engine, instruction, after=()):
            m = Mark(engine)
            for a in after:
                a.used = True
            queues[engine].append((instruction, list(after), m, None))
            return m

        def dmas(name):
            return Dmas(ctx.enter_context(nc.semaphore(name)))

        def dma(group, dst, src, after=(), engine="sync"):
            for a in after:
                a.used = True
            group.n += 1
            queues[engine].append((lambda e: e.dma_start(dst, src), list(after), None, group))

        PE = lambda f, after=(): put("tensor", f, after)
        DVE = lambda f, after=(): put("vector", f, after)
        SC = lambda f, after=(): put("scalar", f, after)
        GP = lambda f, after=(): put("gpsimd", f, after)

        top = [nc.sbuf_base]

        def sb(name, shape, dt=F32):
            size = int(np.prod(shape[1:])) * mybir.dt.size(dt)
            t = nc.alloc_sbuf_tensor_at(name, shape, dt, offset=(top[0] + 31) // 32 * 32)
            top[0] = (top[0] + 31) // 32 * 32 + size
            return t

        psum = ctx.enter_context(nc.psum_tensor("psum", [P, 8, CH], F32))
        readers = {b: [] for b in range(8)}
        X = sb("X", [P, NT, D])
        XT = sb("XT", [P, 2, CH])
        xn = sb("xn", [P, 2, TPC, D])
        stats = sb("stats", [P, NT, 6])
        meanvar = sb("meanvar", [P, NT, 2])
        vareps = sb("vareps", [P, NT])
        rstd = sb("rstd", [P, NT])
        neghalf = sb("neghalf", [P, TPC])
        ident = sb("ident", [P, P])
        identb = sb("identb", [P, P], BF16)
        mirror = sb("mirror", [P, P])
        mask_qk = sb("mask_qk", [P, P], BF16)
        mask_kq = sb("mask_kq", [P, P], BF16)
        cols = sb("cols", [P, NCOL])
        ws3 = sb("ws3", [P, D])
        glu_s = sb("glu_s", [P, 2, HB])
        wide = sb("wide", [P, 5, D])
        wo = sb("wo", [P, D])
        FW = {"w1": (0, HID), "w2": (HID, HID), "h1": (2 * HID, HB * HID), "h2": (2 * HID + HB * HID, HB * HID),
              "w3": (2 * HID + 2 * HB * HID, HB * D)}
        NFW = 2 * HID + 2 * HB * HID + HB * D
        fwh = sb("fwh", [P, NFW], F32R)
        fwl = sb("fwl", [P, NFW], F32R)
        lowmax = sb("lowmax", [P, 1])
        lowall = sb("lowall", [P, 1])
        flag = sb("flag", [P, 1], I32)
        shared = top[0]

        mw = sb("mw", [P, E * D])
        router = sb("router", [P, E])
        ebparts = sb("ebparts", [P, E * D + D], BF16)
        onesb = sb("onesb", [P, P], BF16)
        rows = sb("rows", [P, NROW])
        revidx = sb("revidx", [P, TPC, E])
        lg = sb("lg", [P, TPC, E])
        mx = sb("mx", [P, TPC])
        ex = sb("ex", [P, TPC, E])
        den = sb("den", [P, TPC])
        hot = sb("hot", [P, TPC, E])
        gates = sb("gates", [P, 2, TPC, E])
        half = sb("half", [P, 4, D])
        winT = sb("winT", [P, 2 * D])
        woutT = sb("woutT", [P, D])
        wbT = sb("wbT", [P, S])
        wcT = sb("wcT", [S, D])
        meanw = sb("meanw", [P, P])
        dtc = sb("dtc", [P, 3])
        loga = sb("loga", [P, S])
        rowsA = sb("rowsA", [P, S, D])
        steps = sb("steps", [P, P + 1])
        back = sb("back", [P, 1])
        powers = sb("powers", [P, S, P + 1])
        decay = sb("decay", [P, S, P])
        toep = sb("toep", [P, S, P])
        krow = sb("krow", [1, S, 2 * P])
        carry = sb("carry", [P, S, NT])
        XP = sb("XP", [P, T])
        ZS = sb("ZS", [P, T])
        th = sb("th", [P, 2, CH])
        zb = sb("zb", [P, 2, CH])
        Bt = sb("Bt", [P, S, NT])
        U = sb("U", [P, S * NT])
        H = sb("H", [P, S * NT])
        Ysb = sb("Ysb", [P, NT, S])
        xmT = sb("xmT", [S, T])
        YT = sb("YT", [P, 2, CH])
        fraw = sb("fraw", [P, NFW])
        assert top[0] <= nc.sbuf_usable_end, top[0]

        top[0] = shared
        hidH = sb("hidH", [P, 2, 2, HB, CH], F32R)
        hidL = sb("hidL", [P, 2, 2, HB, CH], F32R)
        inH = sb("inH", [P, 2, CH], F32R)
        inL = sb("inL", [P, 2, CH], F32R)
        fth = sb("fth", [P, 2, CH])
        fa = sb("fa", [P, 2, CH])
        fg = sb("fg", [P, 3, CH])
        fy = sb("fy", [P, TPC, D])
        assert top[0] <= nc.sbuf_usable_end, top[0]

        top[0] = shared
        QS = 4
        ks = sb("ks", [KR + MR, NH, T], BF16)
        qs = sb("qs", [KR + MR, QS, G, CH], BF16)
        qparts = sb("qparts", [P, PARTS, CH], BF16)
        kparts = sb("kparts", [P, PARTS, CH], BF16)
        rope = sb("rope", [P, 2, 2, CH])
        rt = sb("rt", [P, 3, CH])
        vaug = sb("vaug", [P, NT, NH, DK + 1])
        prob = sb("prob", [P, 2, G, CH])
        mpart = sb("mpart", [P, 2, G, TPC, NC])
        mall = sb("mall", [P, 2, TPC, G])
        mneg = sb("mneg", [P, 2, TPC, MR, G], BF16)
        mrow = sb("mrow", [MR * G, 2, CH], BF16)
        cu = sb("cu", [P, CH])
        rl = sb("rl", [P, TPC, G])
        cx = sb("cx", [P, TPC, D])
        cxT = sb("cxT", [P, CH])
        assert top[0] <= nc.sbuf_usable_end, top[0]

        def col(name, n=0):
            return cols[:, COL[name][0] + n:COL[name][0] + n + 1]

        def row(name):
            return rows[:, ROW[name][0]:ROW[name][0] + ROW[name][1]]

        xin = dram["x"].rearrange("(j p) d -> p j d", p=P)
        x_in = [dmas(f"x_in{c}") for c in range(NC)]
        for c in range(NC):
            dma(x_in[c], X[:, TPC * c:TPC * (c + 1), :], xin[:, TPC * c:TPC * (c + 1), :])
            if c == 0:
                ld_first = dmas("ld_first")
                dma(ld_first, ident[:], dram["ident"])
                dma(ld_first, router[:], dram["router_w"])
                dma(ld_first, mw[:], dram["expert_wT"])
        ld_rows = dmas("ld_rows")
        dma(ld_rows, rows[:], dram["rows"].broadcast_to((P, NROW)), engine="scalar")
        ld_cols = dmas("ld_cols")
        dma(ld_cols, cols[:], dram["cols"], engine="scalar")
        ld_idx = dmas("ld_idx")
        dma(ld_idx, revidx[:].rearrange("p t e -> p (t e)"), dram["revidx"].broadcast_to((P, TPC * E)), engine="scalar")
        dma(ld_idx, steps[:], dram["steps"].broadcast_to((P, P + 1)), engine="scalar")
        dma(ld_idx, back[:], dram["back"], engine="scalar")
        ld_ssm = dmas("ld_ssm")
        dma(ld_ssm, winT[:], dram["W_inT"])
        dma(ld_ssm, mirror[:], dram["mirror"])
        dma(ld_ssm, woutT[:], dram["W_outT"])
        dma(ld_ssm, wbT[:], dram["W_BT"])
        dma(ld_ssm, wcT[:], dram["W_CT"])
        ld_att = dmas("ld_att")
        dma(ld_att, wide[:], dram["wide"].rearrange("k p d -> p k d"))
        dma(ld_att, wo[:], dram["WoT"])
        dma(ld_att, identb[:], dram["identb"])
        dma(ld_att, mask_qk[:], dram["mask_qk"])
        dma(ld_att, mask_kq[:], dram["mask_kq"])
        ld_mlp = dmas("ld_mlp")
        dma(ld_mlp, fraw[:], dram["mlp_w"])

        c_half = GP(lambda e: e.memset(neghalf[:], -0.5))
        c_onesb = GP(lambda e: e.memset(onesb[:], 1.0))
        c_mean = GP(lambda e: e.memset(meanw[:], 1.0 / D))
        c_eb0 = GP(lambda e: e.memset(ebparts[:], 0.0))
        c_krow = GP(lambda e: e.memset(krow[:], 0.0))

        xw = [[x_in[c].mark] for c in range(NC)]
        xn_readers = [[], []]
        xt_readers = [[], []]
        slot_of = [0]

        def norm(src, writers, c, after=()):
            slot = slot_of[0] % 2
            slot_of[0] += 1
            j0 = TPC * c
            for t in range(TPC):
                m = DVE(lambda e, t=t: e.bn_stats(stats[:, j0 + t, :], src(t)), writers if t == 0 else ())
            for t in range(TPC):
                m = DVE(lambda e, t=t: e.bn_aggr(meanvar[:, j0 + t, :], stats[:, j0 + t, :]), [m] if t == 0 else ())
            ve = GP(lambda e: e.tensor_scalar(vareps[:, j0:j0 + TPC], meanvar[:, j0:j0 + TPC, 1], EPS, None, ALU.add), [m])
            r = GP(lambda e: e.tensor_tensor(rstd[:, j0:j0 + TPC], vareps[:, j0:j0 + TPC], neghalf[:], ALU.pow), [ve, c_half])
            for t in range(TPC):
                m = DVE(lambda e, t=t: e.tensor_scalar(xn[:, slot, t, :], src(t), meanvar[:, j0 + t, 0:1],
                                                       rstd[:, j0 + t:j0 + t + 1], ALU.subtract, ALU.mult),
                        ([r] + xn_readers[slot]) if t == 0 else ())
            return slot, m

        def turn(slot, m, banks):
            b, free = banks.take()
            for t in range(TPC):
                p = PE(lambda e, t=t: e.transpose(psum[:, b, P * t:P * (t + 1)], xn[:, slot, t, :], ident[:]),
                       ([m, ld_first.mark] + free) if t == 0 else ())
            xn_readers[slot] = [p]
            return b, p

        allb = Banks(list(range(8)), readers)

        def split_bias():
            lo, n = ROW["expert_b"][0], E * D + D
            b = rows[:, lo:lo + n]
            m = c_eb0
            for k, r0 in enumerate((0, 32, 64)):
                part = ebparts[r0:r0 + 1, :]
                src = b[r0:r0 + 1, :]
                for n_part in range(k + 1):
                    m = DVE(lambda e, part=part, src=src: e.tensor_copy(part, src), [m, ld_rows.mark])
                    if n_part < k:
                        m = DVE(lambda e, part=part, src=src: e.tensor_tensor(src, src, part, ALU.subtract), [m])
            return m

        def split_mlp():
            m = [SC(lambda e: e.activation(fwh[:], fraw[:], ACT.Copy), [ld_mlp.mark])]
            m = GP(lambda e: e.tensor_tensor(fwl[:], fraw[:], fwh[:].bitcast(F32), ALU.subtract), m)
            m = DVE(lambda e: e.tensor_reduce(lowmax[:], fwl[:].bitcast(F32), AX.X, ALU.max, apply_absolute_value=True), [m])
            m = GP(lambda e: e.partition_all_reduce(lowall[:], lowmax[:], P, bass.bass_isa.ReduceOp.max), [m])
            return DVE(lambda e: e.tensor_scalar(flag[:], lowall[:], 0.0, None, ALU.is_gt), [m])

        def ssm_params():
            g = {}
            a = SC(lambda e: e.activation(dtc[:, 0:1], col("log_dt"), ACT.Exp), [ld_cols.mark])
            a = DVE(lambda e: e.tensor_scalar(dtc[:, 1:2], dtc[:, 0:1], 1e-4, 1.0, ALU.max, ALU.min), [a])
            b, free = allb.take()
            p = PE(lambda e, b=b: e.matmul(psum[:, b, 0:1], meanw[:], dtc[:, 1:2], start=True, stop=True), [a, c_mean] + free)
            g["dtm"] = DVE(lambda e, b=b: e.tensor_copy(dtc[:, 2:3], psum[:, b, 0:1]), [p])
            allb.give(b, g["dtm"])
            lo, hi = math.log(1e-8), float(np.log(np.float32(1.0 - 1e-8)))
            m = SC(lambda e: e.activation(loga[:], cols[:, COL["A_log"][0]:COL["A_log"][0] + S], ACT.Exp))
            m = DVE(lambda e: e.tensor_scalar(loga[:], loga[:], dtc[:, 1:2], -1.0, ALU.mult, ALU.mult), [m])
            m = DVE(lambda e: e.tensor_scalar(loga[:], loga[:], lo, hi, ALU.max, ALU.min), [m])
            for s in range(S):
                pw = SC(lambda e, s=s: e.activation(powers[:, s, :], steps[:], ACT.Exp, scale=loga[:, s:s + 1]),
                        [m, ld_idx.mark])
            r1 = SC(lambda e: e.activation(rowsA[:].rearrange("p s d -> p (s d)"), row("A_log"), ACT.Exp), [ld_rows.mark])
            rd = SC(lambda e: e.activation(row("log_dt"), row("log_dt"), ACT.Exp))
            rd = GP(lambda e: e.tensor_scalar(row("log_dt"), row("log_dt"), 1e-4, 1.0, ALU.max, ALU.min), [rd])
            rd = GP(lambda e: e.tensor_scalar(row("log_dt"), row("log_dt"), -1.0, None, ALU.mult), [rd])
            r1 = GP(lambda e: e.tensor_tensor(rowsA[:], rowsA[:], row("log_dt").unsqueeze(1).broadcast_to((P, S, D)), ALU.mult),
                    [r1, rd])
            r1 = GP(lambda e: e.tensor_scalar(rowsA[:], rowsA[:], lo, hi, ALU.max, ALU.min), [r1])
            g["decay"] = SC(lambda e: e.activation(decay[:], rowsA[:], ACT.Exp, scale=back[:, 0:1]), [r1])
            for q in range(S * P // CH):
                b, free = allb.take()
                p = PE(lambda e, q=q, b=b: e.matmul(psum[0:1, b, :], meanw[:, 0:1], powers[:, 4 * q:4 * q + 4, 1:P + 1],
                                                    start=True, stop=True), [pw] + free)
                m = DVE(lambda e, q=q, b=b: e.tensor_copy(krow[:, 4 * q:4 * q + 4, 0:P],
                                                          psum[0:1, b, :].rearrange("p (s t) -> p s t", s=4)), [p, c_krow])
                allb.give(b, m)
            scratch = nc.dram_tensor("kernel_rows", [S, 2 * P], F32, kind="Internal").ap()
            k_out, k_in = dmas("k_out"), dmas("k_in")
            dma(k_out, scratch.rearrange("s t -> (s t)").unsqueeze(0), krow[:].rearrange("p s t -> p (s t)"), [m])
            skew = bass.AP(tensor=scratch.tensor, offset=scratch.offset, ap=[[1, P], [2 * P, S], [1, P]])
            dma(k_in, toep[:], skew, [k_out.mark])
            g["toep"] = k_in.mark
            m = GP(lambda e: e.tensor_copy(carry[:], powers[:, :, 0:1].broadcast_to((P, S, NT))), [pw])
            g["carry"] = GP(lambda e: e.memset(carry[:, :, 0:1], 0.0), [m])
            g["pw"] = pw
            return g

        def moe(ebias, work=()):
            work = list(work)
            prepared = {}
            small = [None]

            def prepare(c):
                slot, m = norm(lambda t, c=c: X[:, TPC * c + t, :], xw[c], c)
                b, p = turn(slot, m, allb)
                s2 = c % 2
                xt = SC(lambda e: e.activation(XT[:, s2, :], psum[:, b, :], ACT.Copy), [p] + xt_readers[s2])
                allb.give(b, xt)
                lb, free = allb.take()
                for t in range(TPC):
                    p = PE(lambda e, t=t: e.matmul(psum[:, lb, E * t:E * t + E], XT[:, s2, P * t:P * (t + 1)], router[:],
                                                   start=True, stop=True), ([xt] + free) if t == 0 else ())
                bias = row("router_b").unsqueeze(1).broadcast_to((P, TPC, E))
                full = (P, TPC, E)
                m = DVE(lambda e: e.tensor_tensor(lg[:], psum[:, lb, 0:TPC * E].rearrange("p (t e) -> p t e", e=E), bias, ALU.add),
                        [p, ld_rows.mark])
                allb.give(lb, m)
                m = DVE(lambda e: e.tensor_reduce(mx[:], lg[:], AX.X, ALU.max), [m])
                m = DVE(lambda e: e.tensor_tensor(lg[:], lg[:], mx[:].unsqueeze(2).broadcast_to(full), ALU.subtract), [m])
                x = SC(lambda e: e.activation(ex[:], lg[:], ACT.Exp), [m])
                m = DVE(lambda e: e.scalar_tensor_tensor(hot[:], lg[:], 0.0, revidx[:], ALU.is_ge, ALU.mult), [m, ld_idx.mark])
                m = DVE(lambda e: e.tensor_reduce(mx[:], hot[:], AX.X, ALU.max), [m])
                d = DVE(lambda e: e.tensor_reduce(den[:], ex[:], AX.X, ALU.add), [x])
                m = DVE(lambda e: e.tensor_tensor(hot[:], hot[:], mx[:].unsqueeze(2).broadcast_to(full), ALU.is_equal), [m])
                d = DVE(lambda e: e.reciprocal(den[:], den[:]), [d])
                m = DVE(lambda e: e.scalar_tensor_tensor(gates[:, s2, :, :], hot[:], 0.5, den[:].unsqueeze(2).broadcast_to(full),
                                                         ALU.mult, ALU.mult), [d, m])
                prepared[c] = m

            def experts(c):
                s2 = c % 2
                done = []
                for t in range(TPC):
                    j = TPC * c + t
                    bs, last = [], []
                    for h in range(2):
                        b, free = allb.take()
                        PE(lambda e, b=b, h=h: e.matmul(psum[:, b, :], onesb[:], ebparts[:, CH * h:CH * (h + 1)], start=True, stop=False),
                           free + [ebias, c_onesb])
                        p = PE(lambda e, b=b, h=h, t=t: e.matmul(psum[:, b, :], XT[:, s2, P * t:P * (t + 1)], mw[:, CH * h:CH * (h + 1)],
                                                                 start=False, stop=True))
                        bs.append(b)
                        last.append(p)
                    acc = [X[:, j, :], half[:, 2 * s2 + t % 2, :]]
                    prev = [prepared[c], None]
                    for k in range(4):
                        for h in range(2):
                            e_id = 4 * h + k
                            src = psum[:, bs[h], P * k:P * (k + 1)]
                            gate = gates[:, s2, t, e_id:e_id + 1]
                            w = ([last[h]] if k == 0 else []) + ([prev[h]] if prev[h] else [])
                            if h == 1 and k == 0:
                                w += half_readers.get((s2, t % 2), [])
                                prev[h] = DVE(lambda e, a=acc[h], src=src, gate=gate: e.tensor_scalar(a, src, gate, None, ALU.mult), w)
                            else:
                                prev[h] = DVE(lambda e, a=acc[h], src=src, gate=gate:
                                              e.scalar_tensor_tensor(a, src, gate, a, ALU.mult, ALU.add), w)
                    for h in range(2):
                        allb.give(bs[h], prev[h])
                    m = GP(lambda e, a=acc: e.tensor_tensor(a[0], a[0], a[1], ALU.add), prev)
                    half_readers[(s2, t % 2)] = [m]
                    done.append(m)
                xt_readers[s2] = [last[1]]
                xw[c] = [done[-1]]

            half_readers = {}
            prepare(0)
            for c in range(NC):
                if c + 1 < NC:
                    prepare(c + 1)
                experts(c)
                if c < len(work):
                    work[c]()

        def ssm(g, ebias):
            tails = []
            for c in range(NC):
                s2 = c % 2
                slot, m = norm(lambda t, c=c: X[:, TPC * c + t, :], xw[c], c)
                xw[c] = [GP(lambda e, c=c, slot=slot: e.tensor_tensor(X[:, TPC * c:TPC * (c + 1), :], X[:, TPC * c:TPC * (c + 1), :],
                                                                     xn[:, slot, :, :], ALU.add), [m])]
                xn_readers[slot] = list(xw[c])
                slot2, m = norm(lambda t, slot=slot: xn[:, slot, t, :], [m], c)
                xn_readers[slot] = [m] + xw[c]
                b, p = turn(slot2, m, allb)
                xt = SC(lambda e, b=b, s2=s2: e.activation(XT[:, s2, :], psum[:, b, :], ACT.Identity, bias=col("ln_b"), scale=col("ln_g")),
                        [p, ld_cols.mark] + xt_readers[s2])
                allb.give(b, xt)
                tok = slice(CH * c, CH * (c + 1))
                b, free = allb.take()
                p = PE(lambda e, b=b, s2=s2: e.matmul(psum[:, b, :], winT[:, 0:D], XT[:, s2, :], start=True, stop=True),
                       [xt, ld_ssm.mark] + free)
                xp = SC(lambda e, b=b, tok=tok: e.activation(XP[:, tok], psum[:, b, :], ACT.Identity, bias=col("b_x")), [p])
                allb.give(b, xp)
                b, free = allb.take()
                p = PE(lambda e, b=b, s2=s2: e.matmul(psum[:, b, :], winT[:, D:2 * D], XT[:, s2, :], start=True, stop=True), free)
                xt_readers[s2] = [p]
                z = DVE(lambda e, b=b, s2=s2: e.tensor_scalar(zb[:, s2, :], psum[:, b, :], col("b_z"), None, ALU.add), [p])
                allb.give(b, z)
                tz = SC(lambda e, s2=s2: e.activation(th[:, s2, :], zb[:, s2, :], ACT.Tanh, scale=0.5), [z])
                zs = DVE(lambda e, s2=s2, tok=tok: e.scalar_tensor_tensor(ZS[:, tok], th[:, s2, :], 1.0, zb[:, s2, :], ALU.add, ALU.mult), [tz])
                tails.append((xp, zs))
                if c == 0:
                    bb, bfree = allb.take()
                for t in range(TPC):
                    j = TPC * c + t
                    pb = PE(lambda e, j=j, bb=bb: e.matmul(psum[:, bb, S * j:S * (j + 1)], XP[:, P * j:P * (j + 1)], wbT[:], start=True, stop=True),
                            ([xp] + (bfree if c == 0 else [])) if t == 0 else ())
                if c == 0:
                    hold = allb.ids.index(bb)
                    allb.ids.remove(bb)
            allb.ids.append(bb)
            m = DVE(lambda e: e.tensor_scalar(Bt[:].rearrange("p s j -> p j s"), psum[:, bb, 0:S * NT].rearrange("p (j s) -> p j s", s=S),
                                              dtc[:, 2:3], None, ALU.mult), [pb, g["dtm"]])
            allb.give(bb, m)
            b, free = allb.take()
            for s in range(S):
                p = PE(lambda e, s=s, b=b: e.matmul(psum[:, b, NT * s:NT * (s + 1)], decay[:, s, :], Bt[:, s, :], start=True, stop=True),
                       ([m, g["decay"]] + free) if s == 0 else ())
            u = SC(lambda e, b=b: e.activation(U[:], psum[:, b, 0:S * NT], ACT.Copy, scale=1.0 / D), [p])
            allb.give(b, u)
            h = DVE(lambda e: e.tensor_tensor_scan(H[:], carry[:].rearrange("p s j -> p (s j)"), U[:], 0.0, ALU.mult, ALU.add), [u, g["carry"]])
            b, free = allb.take()
            for s in range(S):
                PE(lambda e, s=s, b=b: e.matmul(psum[:, b, NT * s:NT * (s + 1)], toep[:, s, :], Bt[:, s, :], start=True, stop=False),
                   [g["toep"]] + free)
                p = PE(lambda e, s=s, b=b: e.matmul(psum[:, b, NT * s + 1:NT * (s + 1)], powers[:, s, 0:P], H[:, NT * s:NT * (s + 1) - 1],
                                                    start=False, stop=True), [h])
            y = SC(lambda e, b=b: e.activation(Ysb[:].rearrange("p j s -> p s j"), psum[:, b, 0:S * NT].rearrange("p (s j) -> p s j", s=S), ACT.Copy), [p])
            allb.give(b, y)
            for c in range(NC):
                s2 = c % 2
                tok = slice(CH * c, CH * (c + 1))
                b, free = allb.take()
                for t in range(TPC):
                    p = PE(lambda e, t=t, b=b, c=c: e.matmul(psum[0:S, b, P * t:P * (t + 1)], Ysb[:, TPC * c + t, :], mirror[:], start=True, stop=True),
                           ([y] + free) if t == 0 else ())
                xm = SC(lambda e, b=b, tok=tok: e.activation(xmT[:, tok], psum[0:S, b, :], ACT.Copy), [p])
                allb.give(b, xm)
                b, free = allb.take()
                p = PE(lambda e, b=b, tok=tok: e.matmul(psum[:, b, :], wcT[:], xmT[:, tok], start=True, stop=True), [xm] + free)
                y1 = DVE(lambda e, b=b, tok=tok, s2=s2: e.scalar_tensor_tensor(YT[:, s2, :], XP[:, tok], col("D_skip"), psum[:, b, :], ALU.mult, ALU.add),
                         [p, tails[c][0]] + yt_readers[s2])
                allb.give(b, y1)
                y2 = DVE(lambda e, tok=tok, s2=s2: e.scalar_tensor_tensor(YT[:, s2, :], YT[:, s2, :], 0.5, ZS[:, tok], ALU.mult, ALU.mult),
                         [y1, tails[c][1]])
                b, free = allb.take()
                for t in range(TPC):
                    PE(lambda e, t=t, b=b: e.matmul(psum[:, b, P * t:P * (t + 1)], onesb[:], ebparts[:, E * D:E * D + D], start=True, stop=False),
                       ([y2, ebias] + free) if t == 0 else ())
                    p = PE(lambda e, t=t, b=b, s2=s2: e.matmul(psum[:, b, P * t:P * (t + 1)], YT[:, s2, P * t:P * (t + 1)], woutT[:], start=False, stop=True))
                yt_readers[s2] = [p]
                m = DVE(lambda e, b=b, c=c: e.tensor_tensor(X[:, TPC * c:TPC * (c + 1), :], psum[:, b, :].rearrange("p (t d) -> p t d", t=TPC),
                                                            X[:, TPC * c:TPC * (c + 1), :], ALU.add), [p] + xw[c])
                allb.give(b, m)
                xw[c] = [m]

        yt_readers = [[], []]

        def mlp(fwready, enter, store=None):
            enter = list(enter)
            th_r, a_r, g_r = [[], []], [[], []], [[], [], []]
            in_r, fy_r = [[], []], []
            hid_r = {(l, i): [] for l in range(2) for i in range(2)}
            count = {"th": 0, "g": 0}

            def products(b, cols_, high, low, weights, free, ready, swap=False):
                o = psum[:, b, cols_]
                n = len(weights)

                def mm(e, act, w, start, stop):
                    return e.matmul(o, act, w, start=start, stop=stop) if swap else e.matmul(o, w, act, start=start, stop=stop)

                for k in range(n):
                    PE(lambda e, k=k: mm(e, high[k], fwh[:, weights[k]], k == 0, False), (free + ready) if k == 0 else ())

                def rest(e):
                    with e.If_ne(low_flag[0], zero[0]):
                        for k in range(n):
                            mm(e, high[k], fwl[:, weights[k]], False, False)
                            mm(e, low[k], fwl[:, weights[k]], False, False)

                PE(rest)
                for k in range(n):
                    p = PE(lambda e, k=k: mm(e, low[k], fwh[:, weights[k]], False, k == n - 1))
                return p

            def W(name, kb, ob):
                lo = FW[name][0]
                width = D if name == "w3" else HID
                return slice(lo + kb * width + ob * P, lo + kb * width + ob * P + P)

            def keep(dst, slot, ob, value, m):
                hi = SC(lambda e: e.activation(hidH[:, dst, slot, ob, :], value, ACT.Copy), [m] + (hid_r[(dst, slot)] if ob == 0 else []) + enter)
                return DVE(lambda e: e.tensor_tensor(hidL[:, dst, slot, ob, :], value, hidH[:, dst, slot, ob, :].bitcast(F32), ALU.subtract), [hi] + enter)

            def first(c):
                i = c % 2
                slot, m = norm(lambda t, c=c: X[:, TPC * c + t, :], xw[c], c)
                b, p = turn(slot, m, allb)
                hi = SC(lambda e: e.activation(inH[:, i, :], psum[:, b, :], ACT.Copy), [p] + in_r[i] + enter)
                lo = DVE(lambda e: e.tensor_tensor(inL[:, i, :], psum[:, b, :], inH[:, i, :].bitcast(F32), ALU.subtract), [hi] + enter)
                allb.give(b, lo)
                return lo

            def glu(c, ready):
                i = c % 2
                for ob in range(HB):
                    b1, free = allb.take()
                    p1 = products(b1, slice(0, CH), [inH[:, i, :]], [inL[:, i, :]], [W("w1", 0, ob)], free, [ready, fwready])
                    b2, free = allb.take()
                    p2 = products(b2, slice(0, CH), [inH[:, i, :]], [inL[:, i, :]], [W("w2", 0, ob)], free, [])
                    k = count["th"] % 2
                    count["th"] += 1
                    gk = count["g"] % 3
                    count["g"] += 1
                    t = SC(lambda e, k=k, b1=b1, ob=ob: e.activation(fth[:, k, :], psum[:, b1, :], ACT.Tanh, scale=glu_s[:, 0, ob:ob + 1]), [p1] + th_r[k] + enter)
                    a = DVE(lambda e, k=k, b1=b1: e.scalar_tensor_tensor(fa[:, k, :], fth[:, k, :], 1.0, psum[:, b1, :], ALU.add, ALU.mult), [t] + enter)
                    allb.give(b1, a)
                    th_r[k] = [a]
                    h = DVE(lambda e, k=k, b2=b2, ob=ob, gk=gk: e.scalar_tensor_tensor(fg[:, gk, :], fa[:, k, :], glu_s[:, 1, ob:ob + 1], psum[:, b2, :], ALU.mult, ALU.mult),
                            [a, p2] + g_r[gk])
                    allb.give(b2, h)
                    m = keep(0, i, ob, fg[:, gk, :], h)
                    g_r[gk] = [m]
                in_r[i] = [p2]
                return m

            def layer(name, src, c, ready):
                i = c % 2
                for ob in range(HB):
                    b, free = allb.take()
                    p = products(b, slice(0, CH), [hidH[:, src, i, kb, :] for kb in range(HB)], [hidL[:, src, i, kb, :] for kb in range(HB)],
                                 [W(name, kb, ob) for kb in range(HB)], free, [ready])
                    gk = count["g"] % 3
                    count["g"] += 1
                    g = SC(lambda e, gk=gk, b=b, ob=ob: e.activation(fg[:, gk, :], psum[:, b, :], ACT.Gelu, scale=col(name + "_s", ob)), [p] + g_r[gk])
                    allb.give(b, g)
                    m = keep(1 - src, i, ob, fg[:, gk, :], g)
                    g_r[gk] = [m]
                hid_r[(src, i)] = [p]
                return m

            def last(c, ready):
                i = c % 2
                b, free = allb.take()
                for t in range(TPC):
                    tk = slice(P * t, P * (t + 1))
                    p = products(b, tk, [hidH[:, 0, i, kb, tk] for kb in range(HB)], [hidL[:, 0, i, kb, tk] for kb in range(HB)],
                                 [W("w3", kb, 0) for kb in range(HB)], free if t == 0 else [], [ready] if t == 0 else [], swap=True)
                hid_r[(0, i)] = [p]
                m = DVE(lambda e, b=b: e.tensor_tensor(fy[:], psum[:, b, :].rearrange("p (t d) -> p t d", t=TPC),
                                                       ws3[:].unsqueeze(1).broadcast_to((P, TPC, D)), ALU.mult), [p] + enter + fy_r)
                allb.give(b, m)
                m = DVE(lambda e, c=c: e.tensor_tensor(X[:, TPC * c:TPC * (c + 1), :], X[:, TPC * c:TPC * (c + 1), :], fy[:], ALU.add), [m] + xw[c])
                fy_r[:] = [m]
                xw[c] = [m]
                if store:
                    store(c, m)

            ready = {c: first(c) for c in range(2)}
            for pair in range(NC // 2):
                cs = (2 * pair, 2 * pair + 1)
                for c in cs:
                    ready[c] = glu(c, ready[c])
                for c in cs:
                    ready[c] = layer("h1", 0, c, ready[c])
                for c in cs:
                    ready[c] = layer("h2", 1, c, ready[c])
                if pair + 1 < NC // 2:
                    for c in (2 * pair + 2, 2 * pair + 3):
                        ready[c] = first(c)
                for c in cs:
                    last(c, ready[c])

        def attention(enter):
            enter = list(enter)
            sbanks = Banks([0, 1, 2, 3], readers)
            pvb = 4
            work = Banks([5, 6, 7], readers)
            ones_v = GP(lambda e: e.memset(vaug[:], 1.0), enter)
            k_ones = dmas("k_ones")
            dma(k_ones, ks[KR:KR + MR, :, :].rearrange("p h t -> p (h t)"), dram["ones"].broadcast_to((MR, NH * T)), enter)
            ld_rope = {c: dmas(f"rope{c}") for c in range(NC)}
            k_in = {c: dmas(f"k_rows{c}") for c in range(NC)}
            q_in = {s: dmas(f"q_rows{s}") for s in range(NC * G)}
            m_in = {s: dmas(f"m_rows{s}") for s in range(NC * G)}
            k_out = {c: dmas(f"k_parts{c}") for c in range(NC)}
            q_out = {c: dmas(f"q_parts{c}") for c in range(NC)}
            part_rows = nc.dram_tensor("part_rows", [NC, 2, PARTS, P, CH], BF16, kind="Internal").ap()
            rope_r, kp_r, qp_r, rt_r = [[], []], [], [], [[], []]
            slot_r = {}
            v_done = {}
            b4 = DVE(lambda e: e.memset(psum[:, pvb, :], 0.0), readers[pvb])
            readers[pvb] = [b4]

            def prepare(c):
                i = c % 2
                for k in range(2):
                    dma(ld_rope[c], rope[:, i, k, :], dram["rope"][k, :, CH * c:CH * (c + 1)], enter + rope_r[i])
                slot, m = norm(lambda t, c=c: X[:, TPC * c + t, :], xw[c], c)
                b, p = turn(slot, m, work)
                xt = SC(lambda e, b=b: e.activation(XT[:, i, :], psum[:, b, :], ACT.Copy), [p] + xt_readers[i])
                work.give(b, xt)
                for what in range(2):
                    half_marks = []
                    for k in range(2):
                        b, free = work.take()
                        p = PE(lambda e, b=b, k=k, what=what: e.matmul(psum[:, b, :], wide[:, 2 * what + k, :], XT[:, i, :], start=True, stop=True),
                               [xt, ld_att.mark] + free)
                        m = DVE(lambda e, b=b, k=k: e.tensor_tensor(rt[:, k, :], psum[:, b, :], rope[:, i, k, :], ALU.mult),
                                [p, ld_rope[c].mark] + enter + rt_r[0])
                        work.give(b, m)
                        half_marks.append(m)
                    rope_r[i] = [m]
                    parts = [qparts[:, n, :] if what == 0 else kparts[:, n, :] for n in range(PARTS)]
                    old = qp_r if what == 0 else kp_r
                    m = DVE(lambda e: e.tensor_tensor(rt[:, 2, :], rt[:, 0, :], rt[:, 1, :], ALU.add), half_marks)
                    rt_r[0] = [m]
                    m = DVE(lambda e, parts=parts: e.tensor_copy(parts[0], rt[:, 2, :]), [m] + old)
                    m = DVE(lambda e, parts=parts: e.tensor_tensor(rt[:, 2, :], rt[:, 2, :], parts[0], ALU.subtract), [m])
                    m = DVE(lambda e, parts=parts: e.tensor_copy(parts[1], rt[:, 2, :]), [m])
                    m = DVE(lambda e, parts=parts: e.tensor_tensor(parts[2], rt[:, 2, :], parts[1], ALU.subtract), [m])
                    if what == 1:
                        dma(k_out[c], part_rows[c, 1].rearrange("n p t -> p n t"), kparts[:], [m])
                        for r, (_, n) in enumerate(PAIRS):
                            dma(k_in[c], ks[DK * r:DK * (r + 1), :, CH * c:CH * (c + 1)],
                                part_rows[c, 1, n].rearrange("(h d) t -> d h t", d=DK), [k_out[c].mark])
                        kp_r[:] = [k_out[c].mark]
                    else:
                        dma(q_out[c], part_rows[c, 0].rearrange("n p t -> p n t"), qparts[:], [m])
                        qp_r[:] = [q_out[c].mark]
                b, free = work.take()
                for t in range(TPC):
                    p = PE(lambda e, b=b, t=t: e.matmul(psum[:, b, P * t:P * (t + 1)], XT[:, i, P * t:P * (t + 1)], wide[:, 4, :], start=True, stop=True),
                           free if t == 0 else ())
                xt_readers[i] = [p]
                v = SC(lambda e, b=b: e.activation(vaug[:, TPC * c:TPC * (c + 1), :, 0:DK],
                                                   psum[:, b, :].rearrange("p (t h d) -> p t h d", t=TPC, h=NH), ACT.Copy), [p, ones_v])
                work.give(b, v)
                v_done[c] = v

            def load_q(s):
                c, g = divmod(s, NH // G)
                for r, (n, _) in enumerate(PAIRS):
                    dma(q_in[s], qs[DK * r:DK * (r + 1), s % QS, :, :],
                        part_rows[c, 0, n, G * DK * g:G * DK * (g + 1)].rearrange("(h d) t -> d h t", d=DK),
                        [q_out[c].mark] + enter + slot_r.get(s % QS, []))

            mcount = [0]

            def max_units(s):
                c, g = divmod(s, NH // G)
                i = s % 2
                for hh in range(G):
                    h = G * g + hh
                    for t in range(TPC):
                        keys = P * (TPC * c + t + 1)
                        for k in range(c + 1):
                            n = min(CH, keys - CH * k)
                            diag = k == c
                            b, free = work.take()
                            p = PE(lambda e, b=b, t=t, k=k, n=n, hh=hh, h=h, diag=diag:
                                   e.matmul(psum[:, b, 0:n], qs[0:KR, s % QS, hh, P * t:P * (t + 1)], ks[0:KR, h, CH * k:CH * k + n],
                                            start=True, stop=not diag), free + [q_in[s].mark, k_in[k].mark])
                            if diag:
                                p = PE(lambda e, b=b, n=n: e.matmul(psum[:, b, n - P:n], identb[:], mask_qk[:], start=False, stop=True))
                            m = DVE(lambda e, b=b, n=n, hh=hh, t=t, k=k: e.tensor_reduce(mpart[:, i, hh, t, k:k + 1], psum[:, b, 0:n], AX.X, ALU.max), [p] + enter)
                            work.give(b, m)
                            yield
                m = DVE(lambda e: e.tensor_reduce(mall[:, i, :, :].rearrange("p t h -> p h t"), mpart[:, i, :, :, 0:c + 1], AX.X, ALU.max, negate=True), [m])
                m = DVE(lambda e: e.tensor_copy(mneg[:, i, :, 0, :], mall[:, i, :, :]), [m])
                m = DVE(lambda e: e.tensor_tensor(mneg[:, i, :, 1, :], mall[:, i, :, :], mneg[:, i, :, 0, :], ALU.subtract), [m])
                b, free = work.take()
                pt = psum[:, b, :].bitcast(BF16)
                for t in range(TPC):
                    p = PE(lambda e, t=t: e.transpose(pt[0:MR * G, P * t:P * (t + 1)], mneg[:, i, t, :, :].rearrange("p m h -> p (m h)"), identb[:]),
                           ([m] + free) if t == 0 else ())
                m = DVE(lambda e: e.tensor_copy(mrow[:, i, :], pt[0:MR * G, 0:CH]), [p] + ([m_in[s - 2].mark] if s >= 2 else []))
                work.give(b, m)
                for r in range(MR):
                    dma(m_in[s], qs[KR + r:KR + r + 1, s % QS, :, :], mrow[G * r:G * (r + 1), i, :], [m], engine="gpsimd")

            def exact(s, other, tail):
                c, g = divmod(s, NH // G)
                n_tiles = TPC * (c + 1)
                exps = {}
                pv = None
                total = 4 * (c + 1) * 4
                todo = other_len[0]
                ran = 0

                def scores(k):
                    lo = max(0, k - TPC * c) * P
                    for hh in range(G):
                        h = G * g + hh
                        b, free = sbanks.take()
                        diag = k >= TPC * c
                        p = PE(lambda e, b=b, k=k, h=h, hh=hh, lo=lo, diag=diag:
                               e.matmul(psum[:, b, lo:CH], ks[:, h, P * k:P * (k + 1)], qs[:, s % QS, hh, lo:CH], start=True, stop=not diag),
                               free + [m_in[s].mark, k_ones.mark])
                        if diag:
                            p = PE(lambda e, b=b, lo=lo: e.matmul(psum[:, b, lo:lo + P], identb[:], mask_kq[:], start=False, stop=True))
                        x = SC(lambda e, b=b, k=k, hh=hh, lo=lo: e.activation(prob[:, k % 2, hh, lo:CH], psum[:, b, lo:CH], ACT.Exp, scale=SCALE),
                               [p] + enter + prob_r[k % 2])
                        sbanks.give(b, x)
                        exps[k] = x

                def values(k, first, end):
                    lo = max(0, k - TPC * c) * P
                    for hh in range(G):
                        h = G * g + hh
                        p = PE(lambda e, k=k, h=h, hh=hh, lo=lo, first=first, end=end:
                               e.matmul(psum[32 * hh:32 * hh + DK + 1, pvb, lo:CH], vaug[:, k, h, :], prob[:, k % 2, hh, lo:CH],
                                        start=first, stop=end, skip_group_check=True),
                               [exps[k]] + (readers[pvb] if first else []) + [v_done[k // TPC]])
                    prob_r[k % 2] = [p]
                    return p

                scores(0)
                for k in range(n_tiles):
                    if k + 1 < n_tiles:
                        scores(k + 1)
                    want = (k + 1) * todo // n_tiles
                    while ran < want:
                        if next(other, "end") == "end":
                            break
                        ran += 1
                    pv = values(k, k == 0, k == n_tiles - 1)
                    if k == 1 and tail:
                        tail()
                for _ in other:
                    pass
                slot_r[s % QS] = [pv]
                ev = DVE(lambda e: e.tensor_copy(cu[:], psum[:, pvb, :]), [pv] + cu_r)
                readers[pvb] = [ev]

                def finish():
                    b, free = work.take()
                    for t in range(TPC):
                        p = PE(lambda e, t=t, b=b: e.transpose(psum[:, b, P * t:P * (t + 1)], cu[:, P * t:P * (t + 1)], ident[:]), ([ev] + free) if t == 0 else ())
                    cu_r[:] = [p]
                    view = psum[:, b, :].rearrange("p (t h r) -> p t h r", t=TPC, h=G)
                    m = DVE(lambda e: e.reciprocal(rl[:], view[:, :, :, DK]), [p])
                    m = DVE(lambda e: e.tensor_tensor(cx[:, :, G * g * DK:G * (g + 1) * DK].rearrange("p t (h d) -> p t h d", h=G), view[:, :, :, 0:DK],
                                                      rl[:].unsqueeze(3).broadcast_to((P, TPC, G, DK)), ALU.mult), [m] + (cx_r if g == 0 else []))
                    work.give(b, m)
                    if g < NH // G - 1:
                        return
                    b, free = work.take()
                    for t in range(TPC):
                        p = PE(lambda e, t=t, b=b: e.transpose(psum[:, b, P * t:P * (t + 1)], cx[:, t, :], ident[:]), ([m] + free) if t == 0 else ())
                    cx_r[:] = [p]
                    m = SC(lambda e, b=b: e.activation(cxT[:], psum[:, b, :], ACT.Copy), [p] + cxt_r)
                    work.give(b, m)
                    b, free = work.take()
                    for t in range(TPC):
                        p = PE(lambda e, t=t, b=b: e.matmul(psum[:, b, P * t:P * (t + 1)], cxT[:, P * t:P * (t + 1)], wo[:], start=True, stop=True),
                               ([m] + free) if t == 0 else ())
                    cxt_r[:] = [p]
                    m = DVE(lambda e, b=b: e.tensor_tensor(X[:, TPC * c:TPC * (c + 1), :], psum[:, b, :].rearrange("p (t d) -> p t d", t=TPC),
                                                           X[:, TPC * c:TPC * (c + 1), :], ALU.add), [p] + xw[c])
                    work.give(b, m)
                    xw[c] = [m]

                return finish

            prob_r = [[], []]
            cu_r, cx_r, cxt_r = [], [], []
            other_len = [0]
            n_steps = NC * (NH // G)
            prepare(0)
            load_q(0)
            load_q(1)
            load_q(2)
            for s in range(2):
                for _ in max_units(s):
                    pass
            tail = None
            for s in range(n_steps):
                c, g = divmod(s, NH // G)
                if g == 0 and c + 1 < NC:
                    prepare(c + 1)
                if s + 3 < n_steps:
                    load_q(s + 3)
                if s + 2 < n_steps:
                    other = max_units(s + 2)
                    other_len[0] = 16 * ((s + 2) // G + 1)
                else:
                    other = iter(())
                    other_len[0] = 0
                tail = exact(s, other, tail)
            tail()

        low_flag, zero = [None], [None]
        ebias = split_bias()
        params = {}
        fw = [None]

        def mlp_scales():
            m = DVE(lambda e: e.tensor_scalar(glu_s[:, 0, :], cols[:, COL["w1_s"][0]:COL["w1_s"][0] + HB], 0.5, None, ALU.mult), [ld_cols.mark])
            m = DVE(lambda e: e.tensor_tensor(glu_s[:, 1, :], glu_s[:, 0, :], cols[:, COL["w2_s"][0]:COL["w2_s"][0] + HB], ALU.mult), [m])
            return DVE(lambda e: e.tensor_scalar(ws3[:], row("w3_s"), 0.5, None, ALU.mult), [ld_rows.mark])

        def split():
            fw[0] = split_mlp()

        def prm():
            params.update(ssm_params())

        moe(ebias, [prm, split])
        ssm(params, ebias)
        scales = mlp_scales()
        moe(ebias)
        def read_flag(e):
            low_flag[0] = e.alloc_register("low_part_flag")
            e.reg_load(low_flag[0], flag[0:1, 0:1])
            zero[0] = e.alloc_register("no_low")
            e.reg_mov(zero[0], 0)
        PE(read_flag, [fw[0]])

        def now():
            return [queues_last(n) for n in ("tensor", "vector", "scalar", "gpsimd")]

        def queues_last(n):
            return next(m for _, _, m, _ in reversed(queues[n]) if m is not None)

        last_pe = lambda: next(m for f, _, m, _ in reversed(queues["tensor"]) if m is not None and f is not read_flag)

        def barrier():
            return [last_pe()] + [queues_last(n) for n in ("vector", "scalar", "gpsimd")]

        mlp(scales, barrier())
        attention(barrier())
        y_out = dmas("y_out")
        yv = out.rearrange("b (j p) d -> p (b j) d", p=P)

        def store(c, m):
            dma(y_out, yv[:, TPC * c:TPC * (c + 1), :], X[:, TPC * c:TPC * (c + 1), :], [m])

        mlp(scales, barrier(), store)

        for n in sems:
            k = 0
            for _, _, m, _ in queues[n]:
                if m is not None and m.used:
                    k += 1
                    m.value = k

        block = ctx.enter_context(nc.Block())

        def emit(name, e):
            seen = {}
            for fn, after, m, group in queues[name]:
                for a in after:
                    if isinstance(a.owner, Dmas):
                        key, sem, value = id(a.owner), a.owner.sem, 16 * a.owner.n
                    else:
                        key, sem, value = a.owner, sems[a.owner], a.value
                    if seen.get(key, 0) < value:
                        e.wait_ge(sem, value)
                        seen[key] = value
                i = fn(e)
                if group is not None:
                    i.then_inc(group.sem, 16)
                elif m.used:
                    i.then_inc(sems[name], 1)

        @block.sync
        def _(e):
            emit("sync", e)
            e.wait_ge(y_out.sem, 16 * y_out.n)

        @block.gpsimd
        def _(e):
            emit("gpsimd", e)

        @block.scalar
        def _(e):
            emit("scalar", e)

        @block.vector
        def _(e):
            emit("vector", e)

        @block.tensor
        def _(e):
            emit("tensor", e)


def kernel(**inputs):
    import ml_dtypes
    import concourse.bacc as bacc
    from concourse.bass_utils import run_bass_kernel_spmd as run

    a = {k: np.asarray(v) for k, v in inputs.items()}
    c = np.ascontiguousarray
    arrays = {}
    arrays["x"] = c(a["L0_attn_x"].reshape(T, D))
    arrays["ident"] = np.eye(P, dtype=np.float32)
    arrays["mirror"] = c(np.eye(P, dtype=np.float32)[::-1])
    arrays["identb"] = np.eye(P).astype(ml_dtypes.bfloat16)
    upper = np.triu(np.ones((P, P)), 1) * NEG
    arrays["mask_qk"] = upper.astype(ml_dtypes.bfloat16)
    arrays["mask_kq"] = c(upper.T).astype(ml_dtypes.bfloat16)
    arrays["revidx"] = np.tile(np.arange(E, 0, -1, dtype=np.float32), TPC)[None]
    arrays["steps"] = np.arange(P, -1, -1, dtype=np.float32)[None]
    arrays["back"] = np.arange(P - 1, -1, -1, dtype=np.float32)[:, None]
    arrays["ones"] = np.ones((1, NH * T), ml_dtypes.bfloat16)
    arrays["router_w"] = a["L0_ffn_router_w"]
    arrays["expert_wT"] = c(a["L0_ffn_expert_w"].transpose(1, 0, 2).reshape(D, E * D))
    vec = lambda v: v.reshape(-1, P).T
    arrays["cols"] = c(np.concatenate([
        vec(a["L0_attn_ln_g"]), vec(a["L0_attn_ln_b"]), vec(a["L0_attn_b_in"]), vec(a["L0_attn_D_skip"]), vec(a["L0_attn_log_dt"]),
        vec(a["L1_ffn_w1_s"]), vec(a["L1_ffn_w2_s"]), vec(a["L1_ffn_h1_s"]), vec(a["L1_ffn_h2_s"]), a["L0_attn_A_log"]], axis=1))
    arrays["rows"] = c(np.concatenate([
        a["L0_ffn_router_b"], a["L0_ffn_expert_b"].reshape(-1), a["L0_attn_b_out"], a["L0_attn_log_dt"],
        a["L0_attn_A_log"].T.reshape(-1), a["L1_ffn_w3_s"]])[None])
    arrays["W_inT"] = c(a["L0_attn_W_in"].T)
    arrays["W_outT"] = c(a["L0_attn_W_out"].T)
    arrays["W_BT"] = c(a["L0_attn_W_B"].T)
    arrays["W_CT"] = c(a["L0_attn_W_C"].T)
    swap = np.arange(D) ^ 1
    wq, wk = a["L1_attn_Wq"], a["L1_attn_Wk"]
    arrays["wide"] = c(np.stack([wq.T, wq[swap].T, wk.T, wk[swap].T, a["L1_attn_Wv"].T]))
    arrays["WoT"] = c(a["L1_attn_Wo"].T)
    blocks = lambda w: w.T.reshape(-1, P, w.shape[0]).transpose(1, 0, 2).reshape(P, -1)
    arrays["mlp_w"] = c(np.concatenate([blocks(a[f"L1_ffn_{n}_w"]) for n in ("w1", "w2", "h1", "h2", "w3")], axis=1))
    freq = (np.float32(1.0) / np.float32(10000.0) ** (np.arange(0, DK, 2, dtype=np.float32) / np.float32(DK))).astype(np.float32)
    angle = (np.arange(T, dtype=np.float32)[None, :] * freq[:, None]).astype(np.float32)
    cos, sin = np.cos(angle).astype(np.float32), np.sin(angle).astype(np.float32)
    cos8, sin8 = np.repeat(cos, 2, axis=0), np.stack([-sin, sin], axis=1).reshape(DK, T)
    arrays["rope"] = c(np.stack([np.tile(cos8, (NH, 1)), np.tile(sin8, (NH, 1))]))

    nc = bacc.Bacc("TRN2", target_bir_lowering=False, num_devices=1)
    dram, fed = {}, {}
    for name, v in arrays.items():
        fed[f"in_{name}"] = v
        dram[name] = nc.dram_tensor(f"in_{name}", v.shape, mybir.dt.from_np(v.dtype), kind="ExternalInput").ap()
    out = nc.dram_tensor("out", (1, T, D), F32, kind="ExternalOutput").ap()
    build(nc, dram, out)
    r = run(nc, [fed], core_ids=[0])
    return r.results[0]["out"]
```

```python
import math
from contextlib import ExitStack

import numpy as np

import concourse.bass as bass
from concourse import mybir

F32 = mybir.dt.float32
F32R = mybir.dt.float32r
BF16 = mybir.dt.bfloat16
I32 = mybir.dt.int32
ALU = mybir.AluOpType
ACT = mybir.ActivationFunctionType
AX = mybir.AxisListType

P = 128
T = 2048
D = 128
NT = T // P
CH = 512
NC = T // CH
TPC = CH // P
E = 8
S = 16
HID = 512
HB = HID // P
NH = 16
DK = D // NH
G = 4
EPS = 1e-5
NEG = -1e30
SCALE = 1.0 / math.sqrt(DK)
LAG = 6
PARTS = 3
PAIRS = [(a, b) for a in range(PARTS) for b in range(PARTS)]
KR = len(PAIRS) * DK
MR = 2

COL = {}
for _name, _n in (("ln_g", 1), ("ln_b", 1), ("b_x", 1), ("b_z", 1), ("D_skip", 1), ("log_dt", 1),
                  ("w1_s", HB), ("w2_s", HB), ("h1_s", HB), ("h2_s", HB), ("A_log", S)):
    COL[_name] = (sum(n for _, n in COL.values()), _n)
NCOL = sum(n for _, n in COL.values())
ROW = {}
for _name, _n in (("router_b", E), ("expert_b", E * D), ("b_out", D), ("log_dt", D), ("A_log", S * D), ("w3_s", D)):
    ROW[_name] = (sum(n for _, n in ROW.values()), _n)
NROW = sum(n for _, n in ROW.values())


BIAS_ROWS = (0, 64, 96)


class Mark:

    def __init__(self, owner):
        self.owner, self.used, self.value = owner, False, None


class Dmas:

    def __init__(self, sem):
        self.sem, self.n = sem, 0
        self.mark = Mark(self)


class Banks:

    def __init__(self, ids, readers, state):
        self.ids, self.readers, self.state = ids, readers, state

    def take(self):
        free = [b for b in self.ids if b not in self.state["busy"]]
        b = min(free, key=lambda b: self.state["given"].get(b, -1))
        self.state["busy"].add(b)
        return b, list(self.readers[b])

    def give(self, b, *marks):
        self.state["busy"].discard(b)
        self.state["turn"] += 1
        self.state["given"][b] = self.state["turn"]
        self.readers[b] = list(marks)


def wave(gens, lag):
    gens, turn = list(gens), 0
    live = set(range(len(gens)))
    while live:
        for g in sorted(live):
            if turn >= g * lag and next(gens[g], "end") == "end":
                live.discard(g)
        turn += 1


def in_turn(*steps):
    for one in steps:
        yield from one


def build(nc, dram, out):
    ctx = ExitStack()
    with ctx:
        queues = {n: [] for n in ("tensor", "vector", "scalar", "gpsimd", "sync")}
        sems = {n: ctx.enter_context(nc.semaphore(f"done_{n}")) for n in ("tensor", "vector", "scalar", "gpsimd")}

        def put(engine, instruction, after=(), arms=False):
            m = Mark(engine)
            for a in after:
                a.used = True
            queues[engine].append((instruction, list(after), m, "arms" if arms else None))
            return m

        def dmas(name):
            return Dmas(ctx.enter_context(nc.semaphore(name)))

        def dma(group, dst, src, after=(), engine="sync"):
            for a in after:
                a.used = True
            group.n += 1
            queues[engine].append((lambda e: e.dma_start(dst, src), list(after), None, group))

        PE = lambda f, after=(): put("tensor", f, after)
        DVE = lambda f, after=(): put("vector", f, after)
        SC = lambda f, after=(): put("scalar", f, after)
        GP = lambda f, after=(): put("gpsimd", f, after)

        top = [nc.sbuf_base]

        def sb(name, shape, dt=F32):
            size = int(np.prod(shape[1:])) * mybir.dt.size(dt)
            t = nc.alloc_sbuf_tensor_at(name, shape, dt, offset=(top[0] + 31) // 32 * 32)
            top[0] = (top[0] + 31) // 32 * 32 + size
            return t

        psum = ctx.enter_context(nc.psum_tensor("psum", [P, 8, CH], F32))
        readers = {b: [] for b in range(8)}
        bank_state = {"busy": set(), "given": {}, "turn": 0}
        X = sb("X", [P, NT, D])
        XT = sb("XT", [P, NC, CH])
        xn = sb("xn", [P, NC, TPC, D])
        stats = sb("stats", [P, NT, 6])
        meanvar = sb("meanvar", [P, NT, 2])
        vareps = sb("vareps", [P, NT])
        rstd = sb("rstd", [P, NT])
        neghalf = sb("neghalf", [P, TPC])
        ident = sb("ident", [P, P])
        identb = sb("identb", [P, P], BF16)
        mask_qk = sb("mask_qk", [P, P], BF16)
        mask_kq = sb("mask_kq", [P, P], BF16)
        cols = sb("cols", [P, NCOL])
        ws3 = sb("ws3", [P, D])
        glu_s = sb("glu_s", [P, 2, HB])
        wide = sb("wide", [P, 5, D])
        wo = sb("wo", [P, D])
        FW = {"w1": (0, HID), "w2": (HID, HID), "h1": (2 * HID, HB * HID), "h2": (2 * HID + HB * HID, HB * HID),
              "w3": (2 * HID + 2 * HB * HID, HB * D)}
        NFW = 2 * HID + 2 * HB * HID + HB * D
        NFC = NFW // CH
        fw = sb("fw", [P, NFW], F32R)
        lowmax = sb("lowmax", [P, NFC])
        lowtop = sb("lowtop", [P, 1])
        lowall = sb("lowall", [P, 1])
        flag = sb("flag", [P, 1], I32)
        shared = top[0]

        mirror = sb("mirror", [P, P])
        lowdiff = sb("lowdiff", [P, 2, CH])
        mw = sb("mw", [P, E * D])
        router = sb("router", [P, E])
        ebparts = sb("ebparts", [P, E * D + D], BF16)
        partsel = sb("partsel", [P, P], BF16)
        rows = sb("rows", [P, NROW])
        revidx = sb("revidx", [P, TPC, E])
        lg = sb("lg", [P, NC, TPC, E])
        mx = sb("mx", [P, NC, TPC])
        ex = sb("ex", [P, NC, TPC, E])
        den = sb("den", [P, NC, TPC])
        hot = sb("hot", [P, NC, TPC, E])
        gates = sb("gates", [P, NC, TPC, E])
        half = sb("half", [P, NC, 2, D])
        winT = sb("winT", [P, 2 * D])
        woutT = sb("woutT", [P, D])
        wbT = sb("wbT", [P, S])
        wcT = sb("wcT", [S, D])
        meanw = sb("meanw", [P, P])
        dtc = sb("dtc", [P, 3])
        loga = sb("loga", [P, S])
        rowsA = sb("rowsA", [P, S, D])
        steps = sb("steps", [P, P + 1])
        back = sb("back", [P, 1])
        powers = sb("powers", [P, S, P + 1])
        decay = sb("decay", [P, S, P])
        toep = sb("toep", [P, S, P])
        krow = sb("krow", [1, S, 2 * P])
        carry = sb("carry", [P, S, NT])
        XP = sb("XP", [P, T])
        ZS = sb("ZS", [P, T])
        th = sb("th", [P, NC, CH])
        Bt = sb("Bt", [P, S, NT])
        U = sb("U", [P, S * NT])
        H = sb("H", [P, S * NT])
        Ysb = sb("Ysb", [P, NT, S])
        xmT = sb("xmT", [S, T])
        YT = sb("YT", [P, NC, CH])
        fraw = sb("fraw", [P, NFW])
        assert top[0] <= nc.sbuf_usable_end, top[0]

        top[0] = shared
        hidH = sb("hidH", [P, 2, 2, HB, CH], F32R)
        hidL = sb("hidL", [P, 2, 2, HB, CH], F32R)
        inH = sb("inH", [P, 2, CH], F32R)
        inL = sb("inL", [P, 2, CH], F32R)
        fth = sb("fth", [P, 2, CH])
        fg = sb("fg", [P, 4, CH])
        assert top[0] <= nc.sbuf_usable_end, top[0] - nc.sbuf_usable_end
        top[0] = shared
        QS, PR = 4, 8
        ks = sb("ks", [KR + MR, NH, T], BF16)
        qs = sb("qs", [KR + MR, QS, G, CH], BF16)
        qparts = sb("qparts", [P, PARTS, CH], BF16)
        kparts = sb("kparts", [P, PARTS, CH], BF16)
        rope = sb("rope", [P, 2, 2, CH])
        rt = sb("rt", [P, 2, CH])
        vaug = sb("vaug", [P, NT, NH, DK + 1])
        prob = sb("prob", [P, PR, CH])
        mpart = sb("mpart", [P, 2, G, TPC, NC])
        mall = sb("mall", [P, 2, TPC, G])
        mneg = sb("mneg", [P, 2, TPC, MR, G], BF16)
        mrow = sb("mrow", [MR * G, 2, CH], BF16)
        cu = sb("cu", [P, CH])
        rl = sb("rl", [P, TPC, G])
        cx = sb("cx", [P, TPC, D])
        cxT = sb("cxT", [P, CH])
        assert top[0] <= nc.sbuf_usable_end, top[0] - nc.sbuf_usable_end

        def col(name, n=0):
            return cols[:, COL[name][0] + n:COL[name][0] + n + 1]

        def row(name):
            return rows[:, ROW[name][0]:ROW[name][0] + ROW[name][1]]

        xin = dram["x"].rearrange("(j p) d -> p j d", p=P)
        x_in = [dmas(f"x_in{c}") for c in range(NC)]
        for c in range(NC):
            dma(x_in[c], X[:, TPC * c:TPC * (c + 1), :], xin[:, TPC * c:TPC * (c + 1), :])
            if c == 0:
                ld_first = dmas("ld_first")
                dma(ld_first, ident[:], dram["ident"])
                dma(ld_first, router[:], dram["router_w"])
                dma(ld_first, mw[:], dram["expert_wT"])
        ld_rows = dmas("ld_rows")
        dma(ld_rows, rows[:], dram["rows"].broadcast_to((P, NROW)), engine="scalar")
        ld_cols = dmas("ld_cols")
        dma(ld_cols, cols[:], dram["cols"], engine="scalar")
        ld_idx = dmas("ld_idx")
        dma(ld_idx, revidx[:].rearrange("p t e -> p (t e)"), dram["revidx"].broadcast_to((P, TPC * E)), engine="scalar")
        dma(ld_idx, steps[:], dram["steps"].broadcast_to((P, P + 1)), engine="scalar")
        dma(ld_idx, back[:], dram["back"], engine="scalar")
        ld_ssm = dmas("ld_ssm")
        dma(ld_ssm, winT[:], dram["W_inT"])
        dma(ld_ssm, mirror[:], dram["mirror"])
        dma(ld_ssm, woutT[:], dram["W_outT"])
        dma(ld_ssm, wbT[:], dram["W_BT"])
        dma(ld_ssm, wcT[:], dram["W_CT"])
        ld_att = dmas("ld_att")
        dma(ld_att, wide[:], dram["wide"].rearrange("k p d -> p k d"))
        dma(ld_att, wo[:], dram["WoT"])
        dma(ld_att, identb[:], dram["identb"])
        dma(ld_att, mask_qk[:], dram["mask_qk"])
        dma(ld_att, mask_kq[:], dram["mask_kq"])
        fw_in = dmas("fw_in")
        ld_mlp = dmas("ld_mlp")
        dma(ld_mlp, fraw[:], dram["mlp_w"])

        c_half = GP(lambda e: e.memset(neghalf[:], -0.5))
        dma(ld_idx, partsel[:], dram["partsel"], engine="scalar")
        c_mean = GP(lambda e: e.memset(meanw[:], 1.0 / D))
        c_krow = GP(lambda e: e.memset(krow[:], 0.0))

        xw = [[x_in[c].mark] for c in range(NC)]
        xn_readers = [[] for _ in range(NC)]
        xt_readers = [[] for _ in range(NC)]

        def norm(src, writers, c):
            j0 = TPC * c
            for t in range(TPC):
                m = DVE(lambda e, t=t: e.bn_stats(stats[:, j0 + t, :], src(t)), writers if t == 0 else ())
            yield
            for t in range(TPC):
                m = DVE(lambda e, t=t: e.bn_aggr(meanvar[:, j0 + t, :], stats[:, j0 + t, :]), [m] if t == 0 else ())
            ve = GP(lambda e: e.tensor_scalar(vareps[:, j0:j0 + TPC], meanvar[:, j0:j0 + TPC, 1], EPS, None, ALU.add), [m])
            r = GP(lambda e: e.tensor_tensor(rstd[:, j0:j0 + TPC], vareps[:, j0:j0 + TPC], neghalf[:], ALU.pow), [ve, c_half])
            yield
            yield
            for t in range(TPC):
                m = DVE(lambda e, t=t: e.tensor_scalar(xn[:, c, t, :], src(t), meanvar[:, j0 + t, 0:1],
                                                       rstd[:, j0 + t:j0 + t + 1], ALU.subtract, ALU.mult),
                        ([r] + xn_readers[c]) if t == 0 else ())
            yield
            return m

        def turn(c, m, banks):
            b, free = banks.take()
            for t in range(TPC):
                p = PE(lambda e, t=t: e.transpose(psum[:, b, P * t:P * (t + 1)], xn[:, c, t, :], ident[:]),
                       ([m, ld_first.mark] + free) if t == 0 else ())
            xn_readers[c] = [p]
            return b, p

        allb = Banks(list(range(8)), readers, bank_state)

        def split_bias():
            lo, n = ROW["expert_b"][0], E * D + D
            m = SC(lambda e: e.activation(ebparts[:], rows[:, lo:lo + n], ACT.Copy), [ld_rows.mark])
            for r0 in BIAS_ROWS[1:]:
                m = DVE(lambda e, r0=r0: e.tensor_tensor(rows[r0:P, lo:lo + n], rows[r0:P, lo:lo + n], ebparts[r0:P, :], ALU.subtract), [m])
                m = SC(lambda e, r0=r0: e.activation(ebparts[r0:P, :], rows[r0:P, lo:lo + n], ACT.Copy), [m])
            return m

        def check_mlp_weights():
            rounded = SC(lambda e: e.activation(fw[:], fraw[:], ACT.Copy), [ld_mlp.mark])
            red = [[], []]
            for n in range(NFC):
                i, w = n % 2, slice(CH * n, CH * (n + 1))
                m = GP(lambda e, i=i, w=w: e.tensor_tensor(lowdiff[:, i, :], fraw[:, w], fw[:, w].bitcast(F32), ALU.subtract),
                       [rounded] + red[i])
                m = DVE(lambda e, i=i, n=n: e.tensor_reduce(lowmax[:, n:n + 1], lowdiff[:, i, :], AX.X, ALU.max, apply_absolute_value=True), [m])
                red[i] = [m]
                yield
            dma(fw_in, fw[:].bitcast(F32), fraw[:], red[0] + red[1])
            yield
            m = DVE(lambda e: e.tensor_reduce(lowtop[:], lowmax[:], AX.X, ALU.max), [m])
            m = GP(lambda e: e.partition_all_reduce(lowall[:], lowtop[:], P, bass.bass_isa.ReduceOp.max), [m])
            yield
            flagged[0] = DVE(lambda e: e.tensor_scalar(flag[:], lowall[:], 0.0, None, ALU.is_gt), [m])

        def ssm_params(g):
            lo, hi = math.log(1e-8), float(np.log(np.float32(1.0 - 1e-8)))
            r1 = SC(lambda e: e.activation(rowsA[:].rearrange("p s d -> p (s d)"), row("A_log"), ACT.Exp), [ld_rows.mark])
            rd = SC(lambda e: e.activation(row("log_dt"), row("log_dt"), ACT.Exp))
            rd = DVE(lambda e: e.tensor_scalar(row("log_dt"), row("log_dt"), 1e-4, 1.0, ALU.max, ALU.min), [rd])
            yield
            a = SC(lambda e: e.activation(dtc[:, 0:1], col("log_dt"), ACT.Exp), [ld_cols.mark])
            m = SC(lambda e: e.activation(loga[:], cols[:, COL["A_log"][0]:COL["A_log"][0] + S], ACT.Exp))
            yield
            a = DVE(lambda e: e.tensor_scalar(dtc[:, 1:2], dtc[:, 0:1], 1e-4, 1.0, ALU.max, ALU.min), [a])
            r1 = DVE(lambda e: e.scalar_tensor_tensor(rowsA[:], rowsA[:], -1.0, row("log_dt").unsqueeze(1).broadcast_to((P, S, D)),
                                                      ALU.mult, ALU.mult), [r1, rd])
            yield
            m = DVE(lambda e: e.tensor_scalar(loga[:], loga[:], dtc[:, 1:2], -1.0, ALU.mult, ALU.mult), [m, a])
            r1 = DVE(lambda e: e.tensor_scalar(rowsA[:], rowsA[:], lo, hi, ALU.max, ALU.min), [r1])
            yield
            m = DVE(lambda e: e.tensor_scalar(loga[:], loga[:], lo, hi, ALU.max, ALU.min), [m])
            b, free = allb.take()
            p = PE(lambda e, b=b: e.matmul(psum[:, b, 0:1], meanw[:], dtc[:, 1:2], start=True, stop=True), [a, c_mean] + free)
            g["dtm"] = SC(lambda e, b=b: e.activation(dtc[:, 2:3], psum[:, b, 0:1], ACT.Copy), [p])
            allb.give(b, g["dtm"])
            for s in range(S):
                pw = SC(lambda e, s=s: e.activation(powers[:, s, :], steps[:], ACT.Exp, scale=loga[:, s:s + 1]),
                        [m, ld_idx.mark])
                if s % 2:
                    yield
            g["decay"] = SC(lambda e: e.activation(decay[:], rowsA[:], ACT.Exp, scale=back[:, 0:1]), [r1])
            yield
            for q in range(S * P // CH):
                b, free = allb.take()
                p = PE(lambda e, q=q, b=b: e.matmul(psum[0:1, b, :], meanw[:, 0:1], powers[:, 4 * q:4 * q + 4, 1:P + 1],
                                                    start=True, stop=True), [pw] + free)
                m = SC(lambda e, q=q, b=b: e.activation(krow[:, 4 * q:4 * q + 4, 0:P],
                                                        psum[0:1, b, :].rearrange("p (s t) -> p s t", s=4), ACT.Copy), [p, c_krow])
                allb.give(b, m)
                yield
            scratch = nc.dram_tensor("kernel_rows", [S, 2 * P], F32, kind="Internal").ap()
            k_out, k_in = dmas("k_out"), dmas("k_in")
            dma(k_out, scratch.rearrange("s t -> (s t)").unsqueeze(0), krow[:].rearrange("p s t -> p (s t)"), [m])
            skew = bass.AP(tensor=scratch.tensor, offset=scratch.offset, ap=[[1, P], [2 * P, S], [1, P]])
            dma(k_in, toep[:], skew, [k_out.mark])
            g["toep"] = k_in.mark
            m = GP(lambda e: e.tensor_copy(carry[:], powers[:, :, 0:1].broadcast_to((P, S, NT))), [pw])
            g["carry"] = GP(lambda e: e.memset(carry[:, :, 0:1], 0.0), [m])
            yield

        def moe(c, ebias):
            m = yield from norm(lambda t: X[:, TPC * c + t, :], xw[c], c)
            b, p = turn(c, m, allb)
            yield
            xt = SC(lambda e, b=b: e.activation(XT[:, c, :], psum[:, b, :], ACT.Copy), [p] + xt_readers[c])
            allb.give(b, xt)
            lb, free = allb.take()
            for t in range(TPC):
                p = PE(lambda e, t=t: e.matmul(psum[:, lb, E * t:E * t + E], XT[:, c, P * t:P * (t + 1)], router[:],
                                               start=True, stop=True), ([xt] + free) if t == 0 else ())
            bias = row("router_b").unsqueeze(1).broadcast_to((P, TPC, E))
            full = (P, TPC, E)
            yield
            yield
            m = DVE(lambda e: e.tensor_tensor(lg[:, c, :, :], psum[:, lb, 0:TPC * E].rearrange("p (t e) -> p t e", e=E), bias, ALU.add),
                    [p, ld_rows.mark])
            allb.give(lb, m)
            yield
            m = DVE(lambda e: e.tensor_reduce(mx[:, c, :], lg[:, c, :, :], AX.X, ALU.max), [m])
            yield
            m = DVE(lambda e: e.tensor_tensor(lg[:, c, :, :], lg[:, c, :, :], mx[:, c, :].unsqueeze(2).broadcast_to(full), ALU.subtract), [m])
            x = SC(lambda e: e.activation(ex[:, c, :, :], lg[:, c, :, :], ACT.Exp), [m])
            yield
            m = DVE(lambda e: e.scalar_tensor_tensor(hot[:, c, :, :], lg[:, c, :, :], 0.0, revidx[:], ALU.is_ge, ALU.mult), [m, ld_idx.mark])
            yield
            m = DVE(lambda e: e.tensor_reduce(mx[:, c, :], hot[:, c, :, :], AX.X, ALU.max), [m])
            d = DVE(lambda e: e.tensor_reduce(den[:, c, :], ex[:, c, :, :], AX.X, ALU.add), [x])
            yield
            m = DVE(lambda e: e.tensor_tensor(hot[:, c, :, :], hot[:, c, :, :], mx[:, c, :].unsqueeze(2).broadcast_to(full), ALU.is_equal), [m])
            d = DVE(lambda e: e.reciprocal(den[:, c, :], den[:, c, :]), [d])
            yield
            gated = DVE(lambda e: e.scalar_tensor_tensor(gates[:, c, :, :], hot[:, c, :, :], 0.5, den[:, c, :].unsqueeze(2).broadcast_to(full),
                                                         ALU.mult, ALU.mult), [d, m])
            done = []
            for t in range(TPC):
                j = TPC * c + t
                bs, last = [], []
                for h in range(2):
                    b, free = allb.take()
                    PE(lambda e, b=b, h=h: e.matmul(psum[:, b, :], partsel[:], ebparts[:, CH * h:CH * (h + 1)], start=True, stop=False),
                       free + [ebias, ld_idx.mark])
                    p = PE(lambda e, b=b, h=h, t=t: e.matmul(psum[:, b, :], XT[:, c, P * t:P * (t + 1)], mw[:, CH * h:CH * (h + 1)],
                                                             start=False, stop=True))
                    bs.append(b)
                    last.append(p)
                acc = [X[:, j, :], half[:, c, t % 2, :]]
                prev = [gated, None]
                for k in range(4):
                    for h in range(2):
                        e_id = 4 * h + k
                        src = psum[:, bs[h], P * k:P * (k + 1)]
                        gate = gates[:, c, t, e_id:e_id + 1]
                        w = ([last[h]] if k == 0 else []) + ([prev[h]] if prev[h] else [])
                        if h == 1 and k == 0:
                            w += half_readers.get((c, t % 2), [])
                            prev[h] = DVE(lambda e, a=acc[h], src=src, gate=gate: e.tensor_scalar(a, src, gate, None, ALU.mult), w)
                        else:
                            prev[h] = DVE(lambda e, a=acc[h], src=src, gate=gate:
                                          e.scalar_tensor_tensor(a, src, gate, a, ALU.mult, ALU.add), w)
                    if k < 3:
                        yield
                for h in range(2):
                    allb.give(bs[h], prev[h])
                m = GP(lambda e, a=acc: e.tensor_tensor(a[0], a[0], a[1], ALU.add), prev)
                half_readers[(c, t % 2)] = [m]
                done.append(m)
                yield
            xt_readers[c] = [last[1]]
            xw[c] = [done[-1]]

        half_readers = {}

        ssm_state = {}

        def ssm_front(c):
            tok = slice(CH * c, CH * (c + 1))
            m = yield from norm(lambda t: X[:, TPC * c + t, :], xw[c], c)
            xw[c] = [GP(lambda e: e.tensor_tensor(X[:, TPC * c:TPC * (c + 1), :], X[:, TPC * c:TPC * (c + 1), :],
                                                  xn[:, c, :, :], ALU.add), [m])]
            xn_readers[c] = list(xw[c]) + [m]
            m = yield from norm(lambda t: xn[:, c, t, :], [m], c)
            b, p = turn(c, m, allb)
            yield
            xt = SC(lambda e, b=b: e.activation(XT[:, c, :], psum[:, b, :], ACT.Identity, bias=col("ln_b"), scale=col("ln_g")),
                    [p, ld_cols.mark] + xt_readers[c])
            allb.give(b, xt)
            yield
            b, free = allb.take()
            p = PE(lambda e, b=b: e.matmul(psum[:, b, :], winT[:, 0:D], XT[:, c, :], start=True, stop=True),
                   [xt, ld_ssm.mark] + free)
            xp = SC(lambda e, b=b: e.activation(XP[:, tok], psum[:, b, :], ACT.Identity, bias=col("b_x")), [p])
            allb.give(b, xp)
            b, free = allb.take()
            p = PE(lambda e, b=b: e.matmul(psum[:, b, :], winT[:, D:2 * D], XT[:, c, :], start=True, stop=True), free)
            xt_readers[c] = [p]
            yield
            z = DVE(lambda e, b=b: e.tensor_scalar(ZS[:, tok], psum[:, b, :], col("b_z"), None, ALU.add), [p])
            allb.give(b, z)
            tz = SC(lambda e: e.activation(th[:, c, :], ZS[:, tok], ACT.Tanh, scale=0.5), [z])
            b, free = allb.take()
            for t in range(TPC):
                j = TPC * c + t
                pb = PE(lambda e, j=j, t=t, b=b: e.matmul(psum[:, b, S * t:S * (t + 1)], XP[:, P * j:P * (j + 1)], wbT[:], start=True, stop=True),
                        ([xp] + free) if t == 0 else ())
            yield
            bt = DVE(lambda e, b=b: e.tensor_scalar(Bt[:, :, TPC * c:TPC * (c + 1)].rearrange("p s j -> p j s"),
                                                    psum[:, b, 0:S * TPC].rearrange("p (j s) -> p j s", s=S), dtc[:, 2:3], None, ALU.mult),
                     [pb, params["dtm"]])
            allb.give(b, bt)
            zs = DVE(lambda e: e.scalar_tensor_tensor(ZS[:, tok], th[:, c, :], 1.0, ZS[:, tok], ALU.add, ALU.mult), [tz])
            ssm_state[c] = (xp, zs, bt)
            yield

        def ssm_conv(g):
            m = ssm_state[NC - 1][2]
            b, free = allb.take()
            for s in range(S):
                p = PE(lambda e, s=s, b=b: e.matmul(psum[:, b, NT * s:NT * (s + 1)], decay[:, s, :], Bt[:, s, :], start=True, stop=True),
                       ([m, g["decay"]] + free) if s == 0 else ())
            u = SC(lambda e, b=b: e.activation(U[:], psum[:, b, 0:S * NT], ACT.Copy, scale=1.0 / D), [p])
            allb.give(b, u)
            h = DVE(lambda e: e.tensor_tensor_scan(H[:], carry[:].rearrange("p s j -> p (s j)"), U[:], 0.0, ALU.mult, ALU.add), [u, g["carry"]])
            b, free = allb.take()
            for s in range(S):
                PE(lambda e, s=s, b=b: e.matmul(psum[:, b, NT * s:NT * (s + 1)], toep[:, s, :], Bt[:, s, :], start=True, stop=False),
                   [g["toep"]] + free)
                p = PE(lambda e, s=s, b=b: e.matmul(psum[:, b, NT * s + 1:NT * (s + 1)], powers[:, s, 0:P], H[:, NT * s:NT * (s + 1) - 1],
                                                    start=False, stop=True), [h])
            y = SC(lambda e, b=b: e.activation(Ysb[:].rearrange("p j s -> p s j"), psum[:, b, 0:S * NT].rearrange("p (s j) -> p s j", s=S), ACT.Copy), [p])
            allb.give(b, y)
            ssm_state["y"] = y

        def ssm_tail(c, ebias):
            tok = slice(CH * c, CH * (c + 1))
            xp, zs, _ = ssm_state[c]
            b, free = allb.take()
            for t in range(TPC):
                p = PE(lambda e, t=t, b=b: e.matmul(psum[0:S, b, P * t:P * (t + 1)], Ysb[:, TPC * c + t, :], mirror[:], start=True, stop=True),
                       ([ssm_state["y"]] + free) if t == 0 else ())
            xm = SC(lambda e, b=b: e.activation(xmT[:, tok], psum[0:S, b, :], ACT.Copy), [p])
            allb.give(b, xm)
            yield
            b, free = allb.take()
            p = PE(lambda e, b=b: e.matmul(psum[:, b, :], wcT[:], xmT[:, tok], start=True, stop=True), [xm] + free)
            yield
            y1 = DVE(lambda e, b=b: e.scalar_tensor_tensor(YT[:, c, :], XP[:, tok], col("D_skip"), psum[:, b, :], ALU.mult, ALU.add), [p, xp])
            allb.give(b, y1)
            yield
            y2 = DVE(lambda e: e.scalar_tensor_tensor(YT[:, c, :], YT[:, c, :], 0.5, ZS[:, tok], ALU.mult, ALU.mult), [y1, zs])
            b, free = allb.take()
            for t in range(TPC):
                PE(lambda e, t=t, b=b: e.matmul(psum[:, b, P * t:P * (t + 1)], partsel[:], ebparts[:, E * D:E * D + D], start=True, stop=False),
                   ([y2, ebias] + free) if t == 0 else ())
                p = PE(lambda e, t=t, b=b: e.matmul(psum[:, b, P * t:P * (t + 1)], YT[:, c, P * t:P * (t + 1)], woutT[:], start=False, stop=True))
            yield
            m = DVE(lambda e, b=b: e.tensor_tensor(X[:, TPC * c:TPC * (c + 1), :], psum[:, b, :].rearrange("p (t d) -> p t d", t=TPC),
                                                   X[:, TPC * c:TPC * (c + 1), :], ALU.add), [p] + xw[c])
            allb.give(b, m)
            xw[c] = [m]
            yield

        def W(name, kb, ob):
            width = D if name == "w3" else HID
            lo = FW[name][0] + kb * width + ob * P
            return slice(lo, lo + P)

        mlp_readers = {k: [] for k in [(n, i) for n in ("in", "hid0", "hid1", "th") for i in range(2)] + [("g", i) for i in range(4)]}
        mlp_count = [0]

        def products(jobs, after):
            def arms(e, last):
                def all_jobs(dt):
                    for b, cols_, high, low, weights, swap in jobs:
                        o = psum[:, b, cols_]
                        n = len(weights)
                        for i, (act, w) in enumerate([(x, k) for k in range(n) for x in (high[k], low[k])]):
                            act, wt = (act, fw[:, weights[w]]) if dt is None else (act.bitcast(dt), fw[:, weights[w]].bitcast(dt))
                            lhs, rhs = (act, wt) if swap else (wt, act)
                            m = e.matmul(o, lhs, rhs, start=i == 0, stop=i == 2 * n - 1)
                    last(m)

                with e.If_eq(low_flag[0], zero[0]):
                    all_jobs(None)
                with e.Else():
                    all_jobs(F32)

            return put("tensor", arms, after, arms=True)

        def mlp(c, ring, enter, store=None):
            q = c % 2
            full = slice(0, CH)

            def keep(dst, ob, value, m, engine):
                hi = SC(lambda e: e.activation(hidH[:, dst, q, ob, :], value, ACT.Copy), [m] + (mlp_readers[(f"hid{dst}", q)] if ob == 0 else []))
                return put(engine, lambda e: e.tensor_tensor(hidL[:, dst, q, ob, :], value, hidH[:, dst, q, ob, :].bitcast(F32), ALU.subtract), [hi])

            m = yield from norm(lambda t: X[:, TPC * c + t, :], xw[c], c)
            b, p = turn(c, m, ring)
            hi = SC(lambda e, b=b: e.activation(inH[:, q, :], psum[:, b, :], ACT.Copy), [p] + mlp_readers[("in", q)] + enter)
            ready = DVE(lambda e, b=b: e.tensor_tensor(inL[:, q, :], psum[:, b, :], inH[:, q, :].bitcast(F32), ALU.subtract), [hi])
            ring.give(b, ready)
            yield
            for ob in range(HB):
                b1, free1 = ring.take()
                b2, free2 = ring.take()
                p = products([(b1, full, [inH[:, q, :]], [inL[:, q, :]], [W("w1", 0, ob)], False),
                              (b2, full, [inH[:, q, :]], [inL[:, q, :]], [W("w2", 0, ob)], False)], free1 + free2 + [ready, fw_in.mark])
                gk = mlp_count[0] % 4
                mlp_count[0] += 1
                m = SC(lambda e, b=b1, ob=ob: e.activation(fth[:, ob % 2, :], psum[:, b, :], ACT.Tanh, scale=glu_s[:, 0, ob:ob + 1]), [p] + mlp_readers[("th", ob % 2)] + enter)
                a = DVE(lambda e, b=b1, ob=ob: e.scalar_tensor_tensor(fth[:, ob % 2, :], fth[:, ob % 2, :], 1.0, psum[:, b, :], ALU.add, ALU.mult), [m])
                ring.give(b1, a)
                h = DVE(lambda e, b=b2, ob=ob, gk=gk: e.scalar_tensor_tensor(fg[:, gk, :], fth[:, ob % 2, :], glu_s[:, 1, ob:ob + 1], psum[:, b, :], ALU.mult, ALU.mult),
                        [a, p] + mlp_readers[("g", gk)])
                ring.give(b2, h)
                mlp_readers[("th", ob % 2)] = [h]
                m = keep(0, ob, fg[:, gk, :], h, "gpsimd")
                mlp_readers[("g", gk)] = [m]
            yield
            mlp_readers[("in", q)] = [p]
            for name, src in (("h1", 0), ("h2", 1)):
                ready = m
                for ob in range(HB):
                    b, free = ring.take()
                    p = products([(b, full, [hidH[:, src, q, kb, :] for kb in range(HB)], [hidL[:, src, q, kb, :] for kb in range(HB)],
                                   [W(name, kb, ob) for kb in range(HB)], False)], free + [ready])
                    gk = mlp_count[0] % 4
                    mlp_count[0] += 1
                    g = SC(lambda e, gk=gk, b=b, ob=ob, name=name: e.activation(fg[:, gk, :], psum[:, b, :], ACT.Gelu, scale=col(name + "_s", ob)),
                           [p] + mlp_readers[("g", gk)])
                    ring.give(b, g)
                    m = keep(1 - src, ob, fg[:, gk, :], g, "vector")
                    mlp_readers[("g", gk)] = [m]
                mlp_readers[(f"hid{src}", q)] = [p]
                yield
            b, free = ring.take()
            tiles = [slice(P * t, P * (t + 1)) for t in range(TPC)]
            p = products([(b, tk, [hidH[:, 0, q, kb, tk] for kb in range(HB)], [hidL[:, 0, q, kb, tk] for kb in range(HB)],
                           [W("w3", kb, 0) for kb in range(HB)], True) for tk in tiles], free + [m])
            mlp_readers[("hid0", q)] = [p]
            gk = mlp_count[0] % 4
            mlp_count[0] += 1
            fy = fg[:, gk, :].rearrange("p (t d) -> p t d", t=TPC)
            m = DVE(lambda e, b=b: e.tensor_tensor(fy, psum[:, b, :].rearrange("p (t d) -> p t d", t=TPC),
                                                   ws3[:].unsqueeze(1).broadcast_to((P, TPC, D)), ALU.mult), [p] + mlp_readers[("g", gk)])
            ring.give(b, m)
            yield
            m = DVE(lambda e: e.tensor_tensor(X[:, TPC * c:TPC * (c + 1), :], X[:, TPC * c:TPC * (c + 1), :], fy, ALU.add), [m] + xw[c])
            mlp_readers[("g", gk)] = [m]
            xw[c] = [m]
            if store:
                store(c, m)
            yield

        def mlps(enter, store=None):
            gens = {c: mlp(c, allb, enter, store) for c in range(NC)}
            pre = 5
            for _ in range(pre):
                for c in (0, 1):
                    next(gens[c])
            for pair in range(NC // 2):
                cs = (2 * pair, 2 * pair + 1)
                for stage in range(3):
                    for c in cs:
                        next(gens[c])
                if pair + 1 < NC // 2:
                    for _ in range(pre):
                        for c in (2 * pair + 2, 2 * pair + 3):
                            next(gens[c])
                for c in cs:
                    for _ in gens[c]:
                        pass

        def attention(enter):
            sbanks = Banks([0, 1, 2], readers, bank_state)
            pvb = 3
            mbanks = Banks([4, 5, 6], readers, bank_state)
            side = Banks([7], readers, bank_state)
            ones_v = GP(lambda e: e.memset(vaug[:], 1.0), enter)
            k_ones = dmas("k_ones")
            dma(k_ones, ks[KR:KR + MR, :, :].rearrange("p h t -> p (h t)"), dram["ones"].broadcast_to((MR, NH * T)), enter)
            ld_rope = {c: dmas(f"rope{c}") for c in range(NC)}
            k_in = {c: dmas(f"k_rows{c}") for c in range(NC)}
            q_in = {s: dmas(f"q_rows{s}") for s in range(NC * G)}
            m_in = {s: dmas(f"m_rows{s}") for s in range(NC * G)}
            k_out = {c: dmas(f"k_parts{c}") for c in range(NC)}
            q_out = {c: dmas(f"q_parts{c}") for c in range(NC)}
            part_rows = nc.dram_tensor("part_rows", [NC, 2, PARTS, P, CH], BF16, kind="Internal").ap()
            rope_r, kp_r, qp_r, rt_r = [[], []], [], [], []
            slot_r = {}
            v_done = {}
            b4 = DVE(lambda e: e.memset(psum[:, pvb, :], 0.0), readers[pvb])
            readers[pvb] = [b4]

            def prepare(c, work):
                i = c % 2
                for k in range(2):
                    dma(ld_rope[c], rope[:, i, k, :], dram["rope"][k, :, CH * c:CH * (c + 1)], enter + rope_r[i])
                m = yield from norm(lambda t: X[:, TPC * c + t, :], xw[c], c)
                b, p = turn(c, m, work)
                xt = SC(lambda e, b=b: e.activation(XT[:, c, :], psum[:, b, :], ACT.Copy), [p] + xt_readers[c])
                work.give(b, xt)
                yield
                for what in range(2):
                    parts = [qparts[:, n, :] if what == 0 else kparts[:, n, :] for n in range(PARTS)]
                    old = qp_r if what == 0 else kp_r
                    m = []
                    for k in range(2):
                        b, free = work.take()
                        p = PE(lambda e, b=b, k=k, what=what: e.matmul(psum[:, b, :], wide[:, 2 * what + k, :], XT[:, c, :], start=True, stop=True),
                               [xt, ld_att.mark] + free)
                        m.append(DVE(lambda e, b=b, k=k: e.tensor_tensor(rt[:, k, :], psum[:, b, :], rope[:, i, k, :], ALU.mult),
                                     [p, ld_rope[c].mark] + enter + rt_r))
                        work.give(b, m[-1])
                    if what == 1:
                        rope_r[i] = [m[-1]]
                    yield
                    m = GP(lambda e: e.tensor_tensor(rt[:, 0, :], rt[:, 0, :], rt[:, 1, :], ALU.add), m)
                    m = SC(lambda e, parts=parts: e.activation(parts[0], rt[:, 0, :], ACT.Copy), [m] + old)
                    m = GP(lambda e, parts=parts: e.tensor_tensor(rt[:, 0, :], rt[:, 0, :], parts[0], ALU.subtract), [m])
                    yield
                    m = SC(lambda e, parts=parts: e.activation(parts[1], rt[:, 0, :], ACT.Copy), [m])
                    m = GP(lambda e, parts=parts: e.tensor_tensor(parts[2], rt[:, 0, :], parts[1], ALU.subtract), [m])
                    rt_r[:] = [m]
                    if what == 1:
                        dma(k_out[c], part_rows[c, 1].rearrange("n p t -> p n t"), kparts[:], [m])
                        for r, (_, n) in enumerate(PAIRS):
                            dma(k_in[c], ks[DK * r:DK * (r + 1), :, CH * c:CH * (c + 1)],
                                part_rows[c, 1, n].rearrange("(h d) t -> d h t", d=DK), [k_out[c].mark])
                        kp_r[:] = [k_out[c].mark]
                    else:
                        dma(q_out[c], part_rows[c, 0].rearrange("n p t -> p n t"), qparts[:], [m])
                        qp_r[:] = [q_out[c].mark]
                    yield
                b, free = work.take()
                for t in range(TPC):
                    p = PE(lambda e, b=b, t=t: e.matmul(psum[:, b, P * t:P * (t + 1)], XT[:, c, P * t:P * (t + 1)], wide[:, 4, :], start=True, stop=True),
                           free if t == 0 else ())
                xt_readers[c] = [p]
                v = SC(lambda e, b=b: e.activation(vaug[:, TPC * c:TPC * (c + 1), :, 0:DK],
                                                   psum[:, b, :].rearrange("p (t h d) -> p t h d", t=TPC, h=NH), ACT.Copy), [p, ones_v])
                work.give(b, v)
                v_done[c] = v
                yield

            def load_q(s):
                c, g = divmod(s, NH // G)
                for r, (n, _) in enumerate(PAIRS):
                    dma(q_in[s], qs[DK * r:DK * (r + 1), s % QS, :, :],
                        part_rows[c, 0, n, G * DK * g:G * DK * (g + 1)].rearrange("(h d) t -> d h t", d=DK),
                        [q_out[c].mark] + enter + slot_r.get(s % QS, []))

            mcount = [0]

            def max_units(s):
                c, g = divmod(s, NH // G)
                i = s % 2
                for hh in range(G):
                    h = G * g + hh
                    for t in range(TPC):
                        keys = P * (TPC * c + t + 1)
                        for k in range(c + 1):
                            n = min(CH, keys - CH * k)
                            diag = k == c
                            b, free = mbanks.take()
                            p = PE(lambda e, b=b, t=t, k=k, n=n, hh=hh, h=h, diag=diag:
                                   e.matmul(psum[:, b, 0:n], qs[0:KR, s % QS, hh, P * t:P * (t + 1)], ks[0:KR, h, CH * k:CH * k + n],
                                            start=True, stop=not diag), free + [q_in[s].mark, k_in[k].mark])
                            if diag:
                                p = PE(lambda e, b=b, n=n: e.matmul(psum[:, b, n - P:n], identb[:], mask_qk[:], start=False, stop=True))
                            m = DVE(lambda e, b=b, n=n, hh=hh, t=t, k=k: e.tensor_reduce(mpart[:, i, hh, t, k:k + 1], psum[:, b, 0:n], AX.X, ALU.max), [p] + enter)
                            mbanks.give(b, m)
                            yield
                m = DVE(lambda e: e.tensor_reduce(mall[:, i, :, :].rearrange("p t h -> p h t"), mpart[:, i, :, :, 0:c + 1], AX.X, ALU.max, negate=True), [m])
                m = DVE(lambda e: e.tensor_copy(mneg[:, i, :, 0, :], mall[:, i, :, :]), [m])
                m = DVE(lambda e: e.tensor_tensor(mneg[:, i, :, 1, :], mall[:, i, :, :], mneg[:, i, :, 0, :], ALU.subtract), [m])
                b, free = side.take()
                pt = psum[:, b, :].bitcast(BF16)
                for t in range(TPC):
                    p = PE(lambda e, t=t: e.transpose(pt[0:MR * G, P * t:P * (t + 1)], mneg[:, i, t, :, :].rearrange("p m h -> p (m h)"), identb[:]),
                           ([m] + free) if t == 0 else ())
                m = DVE(lambda e: e.tensor_copy(mrow[:, i, :], pt[0:MR * G, 0:CH]), [p] + ([m_in[s - 2].mark] if s >= 2 else []))
                side.give(b, m)
                for r in range(MR):
                    dma(m_in[s], qs[KR + r:KR + r + 1, s % QS, :, :], mrow[G * r:G * (r + 1), i, :], [m], engine="gpsimd")

            def exact(s, other, side_work, tail):
                c, g = divmod(s, NH // G)
                n_tiles = TPC * (c + 1)
                exps, used = {}, {}

                def scores(k, hh):
                    lo = max(0, k - TPC * c) * P
                    h = G * g + hh
                    b, free = sbanks.take()
                    diag = k >= TPC * c
                    p = PE(lambda e, b=b: e.matmul(psum[:, b, lo:CH], ks[:, h, P * k:P * (k + 1)], qs[:, s % QS, hh, lo:CH], start=True, stop=not diag),
                           free + [m_in[s].mark, k_ones.mark])
                    if diag:
                        p = PE(lambda e, b=b: e.matmul(psum[:, b, lo:lo + P], identb[:], mask_kq[:], start=False, stop=True))
                    i = pr_count[0] % PR
                    pr_count[0] += 1
                    used[(k, hh)] = i
                    x = SC(lambda e, b=b: e.activation(prob[:, i, lo:CH], psum[:, b, lo:CH], ACT.Exp, scale=SCALE), [p] + enter + prob_r[i])
                    sbanks.give(b, x)
                    exps[k] = x

                def values(k):
                    lo = max(0, k - TPC * c) * P
                    first, end = k == 0, k == n_tiles - 1
                    for hh in range(G):
                        h, i = G * g + hh, used[(k, hh)]
                        p = PE(lambda e, h=h, hh=hh, i=i: e.matmul(psum[32 * hh:32 * hh + DK + 1, pvb, lo:CH], vaug[:, k, h, :], prob[:, i, lo:CH],
                                                                   start=first, stop=end, skip_group_check=True),
                               [exps[k]] + (readers[pvb] if first else []) + [v_done[k // TPC]])
                    for hh in range(G):
                        prob_r[used[(k, hh)]] = [p]
                    return p

                for k in range(n_tiles):
                    for hh in range(G):
                        if hh == 2 and k > 0:
                            pv = values(k - 1)
                        scores(k, hh)
                        next(other, None)
                    side_work()
                    if k == 1 and tail:
                        tail()
                pv = values(n_tiles - 1)
                for _ in other:
                    pass
                slot_r[s % QS] = [pv]
                ev = DVE(lambda e: e.tensor_copy(cu[:], psum[:, pvb, :]), [pv] + cu_r)
                readers[pvb] = [ev]

                def finish():
                    b, free = side.take()
                    for t in range(TPC):
                        p = PE(lambda e, t=t, b=b: e.transpose(psum[:, b, P * t:P * (t + 1)], cu[:, P * t:P * (t + 1)], ident[:]), ([ev] + free) if t == 0 else ())
                    cu_r[:] = [p]
                    view = psum[:, b, :].rearrange("p (t h r) -> p t h r", t=TPC, h=G)
                    m = DVE(lambda e: e.reciprocal(rl[:], view[:, :, :, DK]), [p])
                    m = DVE(lambda e: e.tensor_tensor(cx[:, :, G * g * DK:G * (g + 1) * DK].rearrange("p t (h d) -> p t h d", h=G), view[:, :, :, 0:DK],
                                                      rl[:].unsqueeze(3).broadcast_to((P, TPC, G, DK)), ALU.mult), [m] + (cx_r if g == 0 else []))
                    side.give(b, m)
                    if g < NH // G - 1:
                        return
                    b, free = side.take()
                    for t in range(TPC):
                        p = PE(lambda e, t=t, b=b: e.transpose(psum[:, b, P * t:P * (t + 1)], cx[:, t, :], ident[:]), ([m] + free) if t == 0 else ())
                    cx_r[:] = [p]
                    m = SC(lambda e, b=b: e.activation(cxT[:], psum[:, b, :], ACT.Copy), [p] + cxt_r)
                    side.give(b, m)
                    b, free = side.take()
                    for t in range(TPC):
                        p = PE(lambda e, t=t, b=b: e.matmul(psum[:, b, P * t:P * (t + 1)], cxT[:, P * t:P * (t + 1)], wo[:], start=True, stop=True),
                               ([m] + free) if t == 0 else ())
                    cxt_r[:] = [p]
                    m = DVE(lambda e, b=b: e.tensor_tensor(X[:, TPC * c:TPC * (c + 1), :], psum[:, b, :].rearrange("p (t d) -> p t d", t=TPC),
                                                           X[:, TPC * c:TPC * (c + 1), :], ALU.add), [p] + xw[c])
                    side.give(b, m)
                    xw[c] = [m]

                return finish

            prob_r = [[] for _ in range(PR)]
            pr_count = [0]
            cu_r, cx_r, cxt_r = [], [], []
            n_steps = NC * (NH // G)

            def begin():
                load_q(0)
                load_q(1)
                for s in range(2):
                    for _ in max_units(s):
                        pass

            def run():
                tail = None
                for s in range(n_steps):
                    c, g = divmod(s, NH // G)
                    if g == 0:
                        jobs = prepare(c + 1, side) if c + 1 < NC else iter(())

                    def side_work(jobs=jobs):
                        next(jobs, None)

                    if s + 2 < n_steps:
                        if (s + 2) % (NH // G) == 0:
                            for _ in jobs:
                                pass
                        load_q(s + 2)
                        other = max_units(s + 2)
                    else:
                        other = iter(())
                    tail = exact(s, other, side_work, tail)
                tail()

            return prepare, begin, run

        low_flag, zero = [None], [None]
        params, flagged = {}, [None]
        ebias = split_bias()

        def scales_of_mlps():
            m = DVE(lambda e: e.tensor_scalar(glu_s[:, 0, :], cols[:, COL["w1_s"][0]:COL["w1_s"][0] + HB], 0.5, None, ALU.mult), [ld_cols.mark])
            m = DVE(lambda e: e.tensor_tensor(glu_s[:, 1, :], glu_s[:, 0, :], cols[:, COL["w2_s"][0]:COL["w2_s"][0] + HB], ALU.mult), [m])
            return DVE(lambda e: e.tensor_scalar(ws3[:], row("w3_s"), 0.5, None, ALU.mult), [ld_rows.mark])

        wave([in_turn(moe(c, ebias), ssm_front(c)) for c in range(NC)][:1]
             + [in_turn(moe(1, ebias), ssm_front(1)), ssm_params(params)]
             + [in_turn(moe(c, ebias), ssm_front(c)) for c in range(2, NC)] + [check_mlp_weights()], LAG)
        ssm_conv(params)
        wave([in_turn(ssm_tail(c, ebias), moe(c, ebias)) for c in range(NC)], LAG)
        scales = scales_of_mlps()

        def read_flag(e):
            low_flag[0] = e.alloc_register("low_part_flag")
            e.reg_load(low_flag[0], flag[0:1, 0:1])
            zero[0] = e.alloc_register("no_low")
            e.reg_mov(zero[0], 0)

        def barrier():
            return [next(m for f, _, m, _ in reversed(queues[n]) if m is not None and f is not read_flag)
                    for n in ("tensor", "vector", "scalar", "gpsimd")]

        PE(read_flag, [flagged[0]])
        y_out = dmas("y_out")
        yv = out.rearrange("b (j p) d -> p (b j) d", p=P)

        def store(c, m):
            dma(y_out, yv[:, TPC * c:TPC * (c + 1), :], X[:, TPC * c:TPC * (c + 1), :], [m])

        mlps(barrier() + [scales, fw_in.mark])
        prepare, begin, run = attention(barrier())
        for _ in prepare(0, allb):
            pass
        begin()
        run()
        mlps(barrier(), store)

        for n in sems:
            k = 0
            for _, _, m, _ in queues[n]:
                if m is not None and m.used:
                    k += 1
                    m.value = k

        block = ctx.enter_context(nc.Block())

        def emit(name, e):
            seen = {}
            for fn, after, m, group in queues[name]:
                for a in after:
                    if isinstance(a.owner, Dmas):
                        key, sem, value = id(a.owner), a.owner.sem, 16 * a.owner.n
                    else:
                        key, sem, value = a.owner, sems[a.owner], a.value
                    if seen.get(key, 0) < value:
                        e.wait_ge(sem, value)
                        seen[key] = value
                if group == "arms":
                    fn(e, (lambda i: i.then_inc(sems[name], 1)) if m.used else (lambda i: i))
                    continue
                i = fn(e)
                if group is not None:
                    i.then_inc(group.sem, 16)
                elif m.used:
                    i.then_inc(sems[name], 1)

        @block.sync
        def _(e):
            emit("sync", e)
            e.wait_ge(y_out.sem, 16 * y_out.n)

        @block.gpsimd
        def _(e):
            emit("gpsimd", e)

        @block.scalar
        def _(e):
            emit("scalar", e)

        @block.vector
        def _(e):
            emit("vector", e)

        @block.tensor
        def _(e):
            emit("tensor", e)


def kernel(**inputs):
    import ml_dtypes
    import concourse.bacc as bacc
    from concourse.bass_utils import run_bass_kernel_spmd as run

    a = {k: np.asarray(v) for k, v in inputs.items()}
    c = np.ascontiguousarray
    arrays = {}
    arrays["x"] = c(a["L0_attn_x"].reshape(T, D))
    arrays["ident"] = np.eye(P, dtype=np.float32)
    sel = np.zeros((P, P))
    sel[list(BIAS_ROWS)] = 1
    arrays["partsel"] = sel.astype(ml_dtypes.bfloat16)
    arrays["mirror"] = c(np.eye(P, dtype=np.float32)[::-1])
    arrays["identb"] = np.eye(P).astype(ml_dtypes.bfloat16)
    upper = np.triu(np.ones((P, P)), 1) * NEG
    arrays["mask_qk"] = upper.astype(ml_dtypes.bfloat16)
    arrays["mask_kq"] = c(upper.T).astype(ml_dtypes.bfloat16)
    arrays["revidx"] = np.tile(np.arange(E, 0, -1, dtype=np.float32), TPC)[None]
    arrays["steps"] = np.arange(P, -1, -1, dtype=np.float32)[None]
    arrays["back"] = np.arange(P - 1, -1, -1, dtype=np.float32)[:, None]
    arrays["ones"] = np.ones((1, NH * T), ml_dtypes.bfloat16)
    arrays["router_w"] = a["L0_ffn_router_w"]
    arrays["expert_wT"] = c(a["L0_ffn_expert_w"].transpose(1, 0, 2).reshape(D, E * D))
    vec = lambda v: v.reshape(-1, P).T
    arrays["cols"] = c(np.concatenate([
        vec(a["L0_attn_ln_g"]), vec(a["L0_attn_ln_b"]), vec(a["L0_attn_b_in"]), vec(a["L0_attn_D_skip"]), vec(a["L0_attn_log_dt"]),
        vec(a["L1_ffn_w1_s"]), vec(a["L1_ffn_w2_s"]), vec(a["L1_ffn_h1_s"]), vec(a["L1_ffn_h2_s"]), a["L0_attn_A_log"]], axis=1))
    arrays["rows"] = c(np.concatenate([
        a["L0_ffn_router_b"], a["L0_ffn_expert_b"].reshape(-1), a["L0_attn_b_out"], a["L0_attn_log_dt"],
        a["L0_attn_A_log"].T.reshape(-1), a["L1_ffn_w3_s"]])[None])
    arrays["W_inT"] = c(a["L0_attn_W_in"].T)
    arrays["W_outT"] = c(a["L0_attn_W_out"].T)
    arrays["W_BT"] = c(a["L0_attn_W_B"].T)
    arrays["W_CT"] = c(a["L0_attn_W_C"].T)
    swap = np.arange(D) ^ 1
    wq, wk = a["L1_attn_Wq"], a["L1_attn_Wk"]
    arrays["wide"] = c(np.stack([wq.T, wq[swap].T, wk.T, wk[swap].T, a["L1_attn_Wv"].T]))
    arrays["WoT"] = c(a["L1_attn_Wo"].T)
    blocks = lambda w: w.T.reshape(-1, P, w.shape[0]).transpose(1, 0, 2).reshape(P, -1)
    arrays["mlp_w"] = c(np.concatenate([blocks(a[f"L1_ffn_{n}_w"]) for n in ("w1", "w2", "h1", "h2", "w3")], axis=1))
    freq = (np.float32(1.0) / np.float32(10000.0) ** (np.arange(0, DK, 2, dtype=np.float32) / np.float32(DK))).astype(np.float32)
    angle = (np.arange(T, dtype=np.float32)[None, :] * freq[:, None]).astype(np.float32)
    cos, sin = np.cos(angle).astype(np.float32), np.sin(angle).astype(np.float32)
    cos8, sin8 = np.repeat(cos, 2, axis=0), np.stack([-sin, sin], axis=1).reshape(DK, T)
    arrays["rope"] = c(np.stack([np.tile(cos8, (NH, 1)), np.tile(sin8, (NH, 1))]))

    nc = bacc.Bacc("TRN2", target_bir_lowering=False, num_devices=1)
    dram, fed = {}, {}
    for name, v in arrays.items():
        fed[f"in_{name}"] = v
        dram[name] = nc.dram_tensor(f"in_{name}", v.shape, mybir.dt.from_np(v.dtype), kind="ExternalInput").ap()
    out = nc.dram_tensor("out", (1, T, D), F32, kind="ExternalOutput").ap()
    build(nc, dram, out)
    r = run(nc, [fed], core_ids=[0])
    return r.results[0]["out"]
```

```python
import math
from contextlib import ExitStack

import numpy as np

import concourse.bass as bass
from concourse import mybir

F32 = mybir.dt.float32
F32R = mybir.dt.float32r
BF16 = mybir.dt.bfloat16
I32 = mybir.dt.int32
ALU = mybir.AluOpType
ACT = mybir.ActivationFunctionType
AX = mybir.AxisListType

P = 128
T = 2048
D = 128
NT = T // P
CH = 512
NC = T // CH
TPC = CH // P
E = 8
S = 16
HID = 512
HB = HID // P
NH = 16
DK = D // NH
G = 4
EPS = 1e-5
NEG = -1e30
SCALE = 1.0 / math.sqrt(DK)
LAG = 6
PARTS = 3
PAIRS = [(a, b) for a in range(PARTS) for b in range(PARTS)]
KR = len(PAIRS) * DK
LEAD = 0.45
MR = 2

COL = {}
for _name, _n in (("ln_g", 1), ("ln_b", 1), ("b_x", 1), ("b_z", 1), ("D_skip", 1), ("log_dt", 1),
                  ("w1_s", HB), ("w2_s", HB), ("h1_s", HB), ("h2_s", HB), ("w3_s", 1), ("A_log", S)):
    COL[_name] = (sum(n for _, n in COL.values()), _n)
NCOL = sum(n for _, n in COL.values())
ROW = {}
for _name, _n in (("router_b", E), ("expert_b", E * D), ("b_out", D), ("log_dt", D), ("A_log", S * D)):
    ROW[_name] = (sum(n for _, n in ROW.values()), _n)
NROW = sum(n for _, n in ROW.values())


BIAS_ROWS = (0, 64, 96)


class Mark:

    def __init__(self, owner):
        self.owner, self.used, self.value = owner, False, None


class Dmas:

    def __init__(self, sem):
        self.sem, self.n = sem, 0
        self.mark = Mark(self)


class Banks:

    def __init__(self, ids, readers, state):
        self.ids, self.readers, self.state = ids, readers, state

    def take(self):
        free = [b for b in self.ids if b not in self.state["busy"]]
        b = min(free, key=lambda b: self.state["given"].get(b, -1))
        self.state["busy"].add(b)
        return b, list(self.readers[b])

    def give(self, b, *marks):
        self.state["busy"].discard(b)
        self.state["turn"] += 1
        self.state["given"][b] = self.state["turn"]
        self.readers[b] = list(marks)


def wave(entries):
    live, turn = list(entries), 0
    while live:
        live = [(start, g) for start, g in live if turn < start or next(g, "end") != "end"]
        turn += 1


def in_turn(*steps):
    for one in steps:
        yield from one


def build(nc, dram, out):
    ctx = ExitStack()
    with ctx:
        queues = {n: [] for n in ("tensor", "vector", "scalar", "gpsimd", "sync")}
        sems = {n: ctx.enter_context(nc.semaphore(f"done_{n}")) for n in ("tensor", "vector", "scalar", "gpsimd")}

        def put(engine, instruction, after=(), arms=False):
            m = Mark(engine)
            for a in after:
                a.used = True
            queues[engine].append((instruction, list(after), m, "arms" if arms else None))
            return m

        def dmas(name):
            return Dmas(ctx.enter_context(nc.semaphore(name)))

        def dma(group, dst, src, after=(), engine="sync"):
            for a in after:
                a.used = True
            group.n += 1
            queues[engine].append((lambda e: e.dma_start(dst, src), list(after), None, group))

        PE = lambda f, after=(): put("tensor", f, after)
        DVE = lambda f, after=(): put("vector", f, after)
        SC = lambda f, after=(): put("scalar", f, after)
        GP = lambda f, after=(): put("gpsimd", f, after)

        top = [nc.sbuf_base]

        def sb(name, shape, dt=F32):
            size = int(np.prod(shape[1:])) * mybir.dt.size(dt)
            t = nc.alloc_sbuf_tensor_at(name, shape, dt, offset=(top[0] + 31) // 32 * 32)
            top[0] = (top[0] + 31) // 32 * 32 + size
            return t

        psum = ctx.enter_context(nc.psum_tensor("psum", [P, 8, CH], F32))
        readers = {b: [] for b in range(8)}
        bank_state = {"busy": set(), "given": {}, "turn": 0}
        X = sb("X", [P, NT, D])
        XT = sb("XT", [P, NC, CH])
        xn = sb("xn", [P, NC, TPC, D])
        stats = sb("stats", [P, NT, 6])
        meanvar = sb("meanvar", [P, NT, 2])
        vareps = sb("vareps", [P, NT])
        rstd = sb("rstd", [P, NT])
        neghalf = sb("neghalf", [P, TPC])
        ident = sb("ident", [P, P])
        identb = sb("identb", [P, P], BF16)
        mask_qk = sb("mask_qk", [P, P], BF16)
        mask_kq = sb("mask_kq", [P, P], BF16)
        cols = sb("cols", [P, NCOL])
        ws3 = sb("ws3", [P, 1])
        glu_s = sb("glu_s", [P, 2, HB])
        wide = sb("wide", [P, 5, D])
        wo = sb("wo", [P, D])
        FW = {"w1": (0, HID), "w2": (HID, HID), "h1": (2 * HID, HB * HID), "h2": (2 * HID + HB * HID, HB * HID),
              "w3": (2 * HID + 2 * HB * HID, HB * D)}
        NFW = 2 * HID + 2 * HB * HID + HB * D
        NFC = NFW // CH
        fw = sb("fw", [P, NFW], F32R)
        lowmax = sb("lowmax", [P, NFC])
        lowtop = sb("lowtop", [P, 1])
        lowall = sb("lowall", [P, 1])
        flag = sb("flag", [P, 1], I32)
        shared = top[0]

        mirror = sb("mirror", [P, P])
        lowdiff = sb("lowdiff", [P, 2, CH])
        mw = sb("mw", [P, E * D])
        router = sb("router", [P, E])
        ebparts = sb("ebparts", [P, E * D + D], BF16)
        partsel = sb("partsel", [P, P], BF16)
        rows = sb("rows", [P, NROW])
        revidx = sb("revidx", [P, TPC, E])
        lg = sb("lg", [P, NC, TPC, E])
        mx = sb("mx", [P, NC, TPC])
        ex = sb("ex", [P, NC, TPC, E])
        den = sb("den", [P, NC, TPC])
        hot = sb("hot", [P, NC, TPC, E])
        gates = sb("gates", [P, NC, TPC, E])
        half = sb("half", [P, 2, 2, D])
        rest = sb("rest", [P, 2, 2, 2, D])
        winT = sb("winT", [P, 2 * D])
        woutT = sb("woutT", [P, D])
        wbT = sb("wbT", [P, S])
        wcT = sb("wcT", [S, D])
        meanw = sb("meanw", [P, P])
        dtc = sb("dtc", [P, 3])
        loga = sb("loga", [P, S])
        rowsA = sb("rowsA", [P, S, D])
        steps = sb("steps", [P, P + 1])
        back = sb("back", [P, 1])
        powers = sb("powers", [P, S, P + 1])
        decay = sb("decay", [P, S, P])
        toep = sb("toep", [P, S, P])
        krow = sb("krow", [1, S, 2 * P])
        carry = sb("carry", [P, S, NT])
        XP = sb("XP", [P, T])
        ZS = sb("ZS", [P, T])
        th = sb("th", [P, NC, CH])
        Bt = sb("Bt", [P, S, NT])
        U = sb("U", [P, S * NT])
        H = sb("H", [P, S * NT])
        Ysb = sb("Ysb", [P, NT, S])
        xmT = sb("xmT", [S, T])
        YT = sb("YT", [P, NC, CH])
        fraw = sb("fraw", [P, NFW])
        assert top[0] <= nc.sbuf_usable_end, top[0]

        top[0] = shared
        QS, PR = 4, 8
        inH = sb("inH", [P, 2, CH], F32R)
        inL = sb("inL", [P, 2, CH], F32R)
        fth = sb("fth", [P, 2, CH])
        fg = sb("fg", [P, 4, CH])
        ks_early = sb("ks_early", [KR + MR, NC // 2, NH, CH], BF16)
        qs_early = sb("qs_early", [KR + MR, QS // 2, G, CH], BF16)
        qparts = sb("qparts", [P, PARTS, CH], BF16)
        kparts = sb("kparts", [P, PARTS, CH], BF16)
        rope = sb("rope", [P, 2, 2, CH])
        rt = sb("rt", [P, 2, CH])
        vaug = sb("vaug", [P, NT, NH, DK + 1])
        mpart = sb("mpart", [P, 2, G, TPC, NC])
        mall = sb("mall", [P, 2, TPC, G])
        mneg = sb("mneg", [P, 2, TPC, MR, G], BF16)
        mrow = sb("mrow", [MR * G, 2, CH], BF16)
        late = top[0]
        hidH = sb("hidH", [P, 2, 2, HB, CH], F32R)
        hidL = sb("hidL", [P, 2, 2, HB, CH], F32R)
        assert top[0] <= nc.sbuf_usable_end, top[0] - nc.sbuf_usable_end
        top[0] = late
        ks_late = sb("ks_late", [KR + MR, NC // 2, NH, CH], BF16)
        qs_late = sb("qs_late", [KR + MR, QS // 2, G, CH], BF16)
        prob = sb("prob", [P, PR, CH])
        cu = sb("cu", [P, CH])
        rl = sb("rl", [P, TPC, G])
        cx = sb("cx", [P, TPC, D])
        cxT = sb("cxT", [P, CH])
        assert top[0] <= nc.sbuf_usable_end, top[0] - nc.sbuf_usable_end

        ks = [(ks_early, ks_late)[2 * c // NC][:, c % (NC // 2), :, :] for c in range(NC)]
        qs = [(qs_early, qs_late)[2 * i // QS][:, i % (QS // 2), :, :] for i in range(QS)]

        def col(name, n=0):
            return cols[:, COL[name][0] + n:COL[name][0] + n + 1]

        def row(name):
            return rows[:, ROW[name][0]:ROW[name][0] + ROW[name][1]]

        xin = dram["x"].rearrange("(j p) d -> p j d", p=P)
        x_in = [dmas(f"x_in{c}") for c in range(NC)]
        for c in range(NC):
            dma(x_in[c], X[:, TPC * c:TPC * (c + 1), :], xin[:, TPC * c:TPC * (c + 1), :])
            if c == 0:
                ld_first = dmas("ld_first")
                dma(ld_first, ident[:], dram["ident"])
                dma(ld_first, router[:], dram["router_w"])
                dma(ld_first, mw[:], dram["expert_wT"])
        ld_rows = dmas("ld_rows")
        dma(ld_rows, rows[:], dram["rows"].broadcast_to((P, NROW)), engine="scalar")
        ld_cols = dmas("ld_cols")
        dma(ld_cols, cols[:], dram["cols"], engine="scalar")
        ld_idx = dmas("ld_idx")
        dma(ld_idx, revidx[:].rearrange("p t e -> p (t e)"), dram["revidx"].broadcast_to((P, TPC * E)), engine="scalar")
        dma(ld_idx, steps[:], dram["steps"].broadcast_to((P, P + 1)), engine="scalar")
        dma(ld_idx, back[:], dram["back"], engine="scalar")
        ld_ssm = dmas("ld_ssm")
        dma(ld_ssm, winT[:], dram["W_inT"])
        dma(ld_ssm, mirror[:], dram["mirror"])
        dma(ld_ssm, woutT[:], dram["W_outT"])
        dma(ld_ssm, wbT[:], dram["W_BT"])
        dma(ld_ssm, wcT[:], dram["W_CT"])
        ld_att = dmas("ld_att")
        dma(ld_att, wide[:], dram["wide"].rearrange("k p d -> p k d"))
        dma(ld_att, wo[:], dram["WoT"])
        dma(ld_att, identb[:], dram["identb"])
        dma(ld_att, mask_qk[:], dram["mask_qk"])
        dma(ld_att, mask_kq[:], dram["mask_kq"])
        fw_in = dmas("fw_in")
        ld_mlp = dmas("ld_mlp")
        dma(ld_mlp, fraw[:], dram["mlp_w"])

        c_half = GP(lambda e: e.memset(neghalf[:], -0.5))
        dma(ld_idx, partsel[:], dram["partsel"], engine="scalar")
        c_mean = GP(lambda e: e.memset(meanw[:], 1.0 / D))
        c_krow = GP(lambda e: e.memset(krow[:], 0.0))

        xw = [[x_in[c].mark] for c in range(NC)]
        xn_readers = [[] for _ in range(NC)]
        xt_readers = [[] for _ in range(NC)]

        def norm(src, writers, c):
            j0 = TPC * c
            for t in range(TPC):
                m = DVE(lambda e, t=t: e.bn_stats(stats[:, j0 + t, :], src(t)), writers if t == 0 else ())
            yield
            for t in range(TPC):
                m = DVE(lambda e, t=t: e.bn_aggr(meanvar[:, j0 + t, :], stats[:, j0 + t, :]), [m] if t == 0 else ())
            ve = DVE(lambda e: e.tensor_scalar(vareps[:, j0:j0 + TPC], meanvar[:, j0:j0 + TPC, 1], EPS, None, ALU.add), [m])
            r = GP(lambda e: e.tensor_tensor(rstd[:, j0:j0 + TPC], vareps[:, j0:j0 + TPC], neghalf[:], ALU.pow), [ve, c_half])
            yield
            yield
            for t in range(TPC):
                m = DVE(lambda e, t=t: e.tensor_scalar(xn[:, c, t, :], src(t), meanvar[:, j0 + t, 0:1],
                                                       rstd[:, j0 + t:j0 + t + 1], ALU.subtract, ALU.mult),
                        ([r] + xn_readers[c]) if t == 0 else ())
            yield
            return m

        def turn(c, m, banks):
            b, free = banks.take()
            for t in range(TPC):
                p = PE(lambda e, t=t: e.transpose(psum[:, b, P * t:P * (t + 1)], xn[:, c, t, :], ident[:]),
                       ([m, ld_first.mark] + free) if t == 0 else ())
            xn_readers[c] = [p]
            return b, p

        allb = Banks(list(range(8)), readers, bank_state)

        def split_bias():
            lo, n = ROW["expert_b"][0], E * D + D
            m = SC(lambda e: e.activation(ebparts[:], rows[:, lo:lo + n], ACT.Copy), [ld_rows.mark])
            yield
            for r0 in BIAS_ROWS[1:]:
                m = DVE(lambda e, r0=r0: e.tensor_tensor(rows[r0:P, lo:lo + n], rows[r0:P, lo:lo + n], ebparts[r0:P, :], ALU.subtract), [m])
                m = SC(lambda e, r0=r0: e.activation(ebparts[r0:P, :], rows[r0:P, lo:lo + n], ACT.Copy), [m])
                yield
            ebias[:] = [m]

        def check_mlp_weights():
            rounded = SC(lambda e: e.activation(fw[:], fraw[:], ACT.Copy), [ld_mlp.mark])
            red = [[], []]
            for n in range(NFC):
                i, w = n % 2, slice(CH * n, CH * (n + 1))
                m = GP(lambda e, i=i, w=w: e.tensor_tensor(lowdiff[:, i, :], fraw[:, w], fw[:, w].bitcast(F32), ALU.subtract),
                       [rounded] + red[i])
                m = DVE(lambda e, i=i, n=n: e.tensor_reduce(lowmax[:, n:n + 1], lowdiff[:, i, :], AX.X, ALU.max, apply_absolute_value=True), [m])
                red[i] = [m]
                yield
            dma(fw_in, fw[:].bitcast(F32), fraw[:], red[0] + red[1])
            yield
            m = DVE(lambda e: e.tensor_reduce(lowtop[:], lowmax[:], AX.X, ALU.max), [m])
            m = GP(lambda e: e.partition_all_reduce(lowall[:], lowtop[:], P, bass.bass_isa.ReduceOp.max), [m])
            yield
            flagged[0] = DVE(lambda e: e.tensor_scalar(flag[:], lowall[:], 0.0, None, ALU.is_gt), [m])

        def ssm_params(g):
            lo, hi = math.log(1e-8), float(np.log(np.float32(1.0 - 1e-8)))
            r1 = SC(lambda e: e.activation(rowsA[:].rearrange("p s d -> p (s d)"), row("A_log"), ACT.Exp), [ld_rows.mark])
            rd = SC(lambda e: e.activation(row("log_dt"), row("log_dt"), ACT.Exp))
            rd = DVE(lambda e: e.tensor_scalar(row("log_dt"), row("log_dt"), 1e-4, 1.0, ALU.max, ALU.min), [rd])
            yield
            a = SC(lambda e: e.activation(dtc[:, 0:1], col("log_dt"), ACT.Exp), [ld_cols.mark])
            m = SC(lambda e: e.activation(loga[:], cols[:, COL["A_log"][0]:COL["A_log"][0] + S], ACT.Exp))
            yield
            a = DVE(lambda e: e.tensor_scalar(dtc[:, 1:2], dtc[:, 0:1], 1e-4, 1.0, ALU.max, ALU.min), [a])
            r1 = DVE(lambda e: e.scalar_tensor_tensor(rowsA[:], rowsA[:], -1.0, row("log_dt").unsqueeze(1).broadcast_to((P, S, D)),
                                                      ALU.mult, ALU.mult), [r1, rd])
            yield
            m = DVE(lambda e: e.tensor_scalar(loga[:], loga[:], dtc[:, 1:2], -1.0, ALU.mult, ALU.mult), [m, a])
            r1 = DVE(lambda e: e.tensor_scalar(rowsA[:], rowsA[:], lo, hi, ALU.max, ALU.min), [r1])
            yield
            m = DVE(lambda e: e.tensor_scalar(loga[:], loga[:], lo, hi, ALU.max, ALU.min), [m])
            b, free = allb.take()
            p = PE(lambda e, b=b: e.matmul(psum[:, b, 0:1], meanw[:], dtc[:, 1:2], start=True, stop=True), [a, c_mean] + free)
            g["dtm"] = SC(lambda e, b=b: e.activation(dtc[:, 2:3], psum[:, b, 0:1], ACT.Copy), [p])
            allb.give(b, g["dtm"])
            for s in range(S):
                pw = SC(lambda e, s=s: e.activation(powers[:, s, :], steps[:], ACT.Exp, scale=loga[:, s:s + 1]),
                        [m, ld_idx.mark])
                if s % 2:
                    yield
            g["decay"] = SC(lambda e: e.activation(decay[:], rowsA[:], ACT.Exp, scale=back[:, 0:1]), [r1])
            yield
            for q in range(S * P // CH):
                b, free = allb.take()
                p = PE(lambda e, q=q, b=b: e.matmul(psum[0:1, b, :], meanw[:, 0:1], powers[:, 4 * q:4 * q + 4, 1:P + 1],
                                                    start=True, stop=True), [pw] + free)
                m = SC(lambda e, q=q, b=b: e.activation(krow[:, 4 * q:4 * q + 4, 0:P],
                                                        psum[0:1, b, :].rearrange("p (s t) -> p s t", s=4), ACT.Copy), [p, c_krow])
                allb.give(b, m)
                yield
            scratch = nc.dram_tensor("kernel_rows", [S, 2 * P], F32, kind="Internal").ap()
            k_out, k_in = dmas("k_out"), dmas("k_in")
            dma(k_out, scratch.rearrange("s t -> (s t)").unsqueeze(0), krow[:].rearrange("p s t -> p (s t)"), [m])
            skew = bass.AP(tensor=scratch.tensor, offset=scratch.offset, ap=[[1, P], [2 * P, S], [1, P]])
            dma(k_in, toep[:], skew, [k_out.mark])
            g["toep"] = k_in.mark
            m = GP(lambda e: e.tensor_copy(carry[:], powers[:, :, 0:1].broadcast_to((P, S, NT))), [pw])
            g["carry"] = GP(lambda e: e.memset(carry[:, :, 0:1], 0.0), [m])
            yield

        def moe(c, ebias):
            m = yield from norm(lambda t: X[:, TPC * c + t, :], xw[c], c)
            b, p = turn(c, m, allb)
            yield
            xt = SC(lambda e, b=b: e.activation(XT[:, c, :], psum[:, b, :], ACT.Copy), [p] + xt_readers[c])
            allb.give(b, xt)
            lb, free = allb.take()
            for t in range(TPC):
                p = PE(lambda e, t=t: e.matmul(psum[:, lb, E * t:E * t + E], XT[:, c, P * t:P * (t + 1)], router[:],
                                               start=True, stop=True), ([xt] + free) if t == 0 else ())
            bias = row("router_b").unsqueeze(1).broadcast_to((P, TPC, E))
            full = (P, TPC, E)
            yield
            yield
            m = DVE(lambda e: e.tensor_tensor(lg[:, c, :, :], psum[:, lb, 0:TPC * E].rearrange("p (t e) -> p t e", e=E), bias, ALU.add),
                    [p, ld_rows.mark])
            allb.give(lb, m)
            yield
            m = DVE(lambda e: e.tensor_reduce(mx[:, c, :], lg[:, c, :, :], AX.X, ALU.max), [m])
            yield
            m = DVE(lambda e: e.tensor_tensor(lg[:, c, :, :], lg[:, c, :, :], mx[:, c, :].unsqueeze(2).broadcast_to(full), ALU.subtract), [m])
            x = SC(lambda e: e.activation(ex[:, c, :, :], lg[:, c, :, :], ACT.Exp), [m])
            yield
            m = DVE(lambda e: e.scalar_tensor_tensor(hot[:, c, :, :], lg[:, c, :, :], 0.0, revidx[:], ALU.is_ge, ALU.mult), [m, ld_idx.mark])
            yield
            m = DVE(lambda e: e.tensor_reduce(mx[:, c, :], hot[:, c, :, :], AX.X, ALU.max), [m])
            d = DVE(lambda e: e.tensor_reduce(den[:, c, :], ex[:, c, :, :], AX.X, ALU.add), [x])
            yield
            m = DVE(lambda e: e.tensor_tensor(hot[:, c, :, :], hot[:, c, :, :], mx[:, c, :].unsqueeze(2).broadcast_to(full), ALU.is_equal), [m])
            d = DVE(lambda e: e.reciprocal(den[:, c, :], den[:, c, :]), [d])
            yield
            gated = DVE(lambda e: e.scalar_tensor_tensor(gates[:, c, :, :], hot[:, c, :, :], 0.5, den[:, c, :].unsqueeze(2).broadcast_to(full),
                                                         ALU.mult, ALU.mult), [d, m])
            done = []
            for t in range(TPC):
                j = TPC * c + t
                bs, last = [], []
                for h in range(2):
                    b, free = allb.take()
                    PE(lambda e, b=b, h=h: e.matmul(psum[:, b, :], partsel[:], ebparts[:, CH * h:CH * (h + 1)], start=True, stop=False),
                       free + ebias + [ld_idx.mark])
                    p = PE(lambda e, b=b, h=h, t=t: e.matmul(psum[:, b, :], XT[:, c, P * t:P * (t + 1)], mw[:, CH * h:CH * (h + 1)],
                                                             start=False, stop=True))
                    bs.append(b)
                    last.append(p)
                x_sum, half_sum, rest_sum, other = X[:, j, :], half[:, c % 2, t % 2, :], rest[:, c % 2, t % 2, 0, :], rest[:, c % 2, t % 2, 1, :]

                def start(to, h, k, after):
                    return SC(lambda e, t=t, h=h, k=k, b=bs[h]: e.activation(to, psum[:, b, P * k:P * (k + 1)], ACT.Copy,
                                                                           scale=gates[:, c, t, 4 * h + k:4 * h + k + 1]), [last[h]] + list(after))

                def add(to, h, k, after):
                    return DVE(lambda e, t=t, h=h, k=k, b=bs[h]: e.scalar_tensor_tensor(to, psum[:, b, P * k:P * (k + 1)],
                                                                                      gates[:, c, t, 4 * h + k:4 * h + k + 1], to, ALU.mult, ALU.add),
                               [last[h]] + after)

                old = half_readers.get((c % 2, t % 2), [])
                c1 = start(rest_sum, 0, 3, old + [gated])
                b1 = start(half_sum, 1, 0, ())
                c2 = start(other, 1, 3, ())
                a1 = add(x_sum, 0, 0, [c1] + xw[c])
                b1 = add(half_sum, 1, 1, [b1, c2])
                yield
                a1 = add(x_sum, 0, 1, [a1])
                b1 = add(half_sum, 1, 2, [b1])
                c1 = GP(lambda e, a=rest_sum, b=other: e.tensor_tensor(a, a, b, ALU.add), [c2])
                yield
                a1 = add(x_sum, 0, 2, [a1])
                allb.give(bs[0], a1)
                allb.give(bs[1], b1)
                m = GP(lambda e, a=half_sum, b=rest_sum: e.tensor_tensor(a, a, b, ALU.add), [b1, c1])
                m = GP(lambda e, a=x_sum, b=half_sum: e.tensor_tensor(a, a, b, ALU.add), [a1, m])
                half_readers[(c % 2, t % 2)] = [m]
                done.append(m)
                yield
            xt_readers[c] = [last[1]]
            xw[c] = [done[-1]]

        half_readers = {}

        ssm_state = {}

        def ssm_front(c):
            tok = slice(CH * c, CH * (c + 1))
            m = yield from norm(lambda t: X[:, TPC * c + t, :], xw[c], c)
            xw[c] = [GP(lambda e: e.tensor_tensor(X[:, TPC * c:TPC * (c + 1), :], X[:, TPC * c:TPC * (c + 1), :],
                                                  xn[:, c, :, :], ALU.add), [m])]
            xn_readers[c] = list(xw[c]) + [m]
            m = yield from norm(lambda t: xn[:, c, t, :], [m], c)
            b, p = turn(c, m, allb)
            yield
            xt = SC(lambda e, b=b: e.activation(XT[:, c, :], psum[:, b, :], ACT.Identity, bias=col("ln_b"), scale=col("ln_g")),
                    [p, ld_cols.mark] + xt_readers[c])
            allb.give(b, xt)
            yield
            b, free = allb.take()
            p = PE(lambda e, b=b: e.matmul(psum[:, b, :], winT[:, 0:D], XT[:, c, :], start=True, stop=True),
                   [xt, ld_ssm.mark] + free)
            xp = SC(lambda e, b=b: e.activation(XP[:, tok], psum[:, b, :], ACT.Identity, bias=col("b_x")), [p])
            allb.give(b, xp)
            b, free = allb.take()
            p = PE(lambda e, b=b: e.matmul(psum[:, b, :], winT[:, D:2 * D], XT[:, c, :], start=True, stop=True), free)
            xt_readers[c] = [p]
            yield
            z = DVE(lambda e, b=b: e.tensor_scalar(ZS[:, tok], psum[:, b, :], col("b_z"), None, ALU.add), [p])
            allb.give(b, z)
            tz = SC(lambda e: e.activation(th[:, c, :], ZS[:, tok], ACT.Tanh, scale=0.5), [z])
            b, free = allb.take()
            for t in range(TPC):
                j = TPC * c + t
                pb = PE(lambda e, j=j, t=t, b=b: e.matmul(psum[:, b, S * t:S * (t + 1)], XP[:, P * j:P * (j + 1)], wbT[:], start=True, stop=True),
                        ([xp] + free) if t == 0 else ())
            yield
            bt = DVE(lambda e, b=b: e.tensor_scalar(Bt[:, :, TPC * c:TPC * (c + 1)].rearrange("p s j -> p j s"),
                                                    psum[:, b, 0:S * TPC].rearrange("p (j s) -> p j s", s=S), dtc[:, 2:3], None, ALU.mult),
                     [pb, params["dtm"]])
            allb.give(b, bt)
            zs = DVE(lambda e: e.scalar_tensor_tensor(ZS[:, tok], th[:, c, :], 1.0, ZS[:, tok], ALU.add, ALU.mult), [tz])
            ssm_state[c] = (xp, zs, bt)
            yield

        def ssm_conv(g):
            m = ssm_state[NC - 1][2]
            b, free = allb.take()
            for s in range(S):
                p = PE(lambda e, s=s, b=b: e.matmul(psum[:, b, NT * s:NT * (s + 1)], decay[:, s, :], Bt[:, s, :], start=True, stop=True),
                       ([m, g["decay"]] + free) if s == 0 else ())
            yield
            u = SC(lambda e, b=b: e.activation(U[:], psum[:, b, 0:S * NT], ACT.Copy, scale=1.0 / D), [p])
            allb.give(b, u)
            h = DVE(lambda e: e.tensor_tensor_scan(H[:], carry[:].rearrange("p s j -> p (s j)"), U[:], 0.0, ALU.mult, ALU.add), [u, g["carry"]])
            yield
            b, free = allb.take()
            for s in range(S):
                PE(lambda e, s=s, b=b: e.matmul(psum[:, b, NT * s:NT * (s + 1)], toep[:, s, :], Bt[:, s, :], start=True, stop=False),
                   [g["toep"]] + free)
                p = PE(lambda e, s=s, b=b: e.matmul(psum[:, b, NT * s + 1:NT * (s + 1)], powers[:, s, 0:P], H[:, NT * s:NT * (s + 1) - 1],
                                                    start=False, stop=True), [h])
            y = SC(lambda e, b=b: e.activation(Ysb[:].rearrange("p j s -> p s j"), psum[:, b, 0:S * NT].rearrange("p (s j) -> p s j", s=S), ACT.Copy), [p])
            allb.give(b, y)
            ssm_state["y"] = y

        def ssm_tail(c, ebias):
            tok = slice(CH * c, CH * (c + 1))
            xp, zs, _ = ssm_state[c]
            b, free = allb.take()
            for t in range(TPC):
                p = PE(lambda e, t=t, b=b: e.matmul(psum[0:S, b, P * t:P * (t + 1)], Ysb[:, TPC * c + t, :], mirror[:], start=True, stop=True),
                       ([ssm_state["y"]] + free) if t == 0 else ())
            xm = SC(lambda e, b=b: e.activation(xmT[:, tok], psum[0:S, b, :], ACT.Copy), [p])
            allb.give(b, xm)
            yield
            b, free = allb.take()
            p = PE(lambda e, b=b: e.matmul(psum[:, b, :], wcT[:], xmT[:, tok], start=True, stop=True), [xm] + free)
            yield
            y1 = DVE(lambda e, b=b: e.scalar_tensor_tensor(YT[:, c, :], XP[:, tok], col("D_skip"), psum[:, b, :], ALU.mult, ALU.add), [p, xp])
            allb.give(b, y1)
            yield
            y2 = DVE(lambda e: e.scalar_tensor_tensor(YT[:, c, :], YT[:, c, :], 0.5, ZS[:, tok], ALU.mult, ALU.mult), [y1, zs])
            b, free = allb.take()
            for t in range(TPC):
                PE(lambda e, t=t, b=b: e.matmul(psum[:, b, P * t:P * (t + 1)], partsel[:], ebparts[:, E * D:E * D + D], start=True, stop=False),
                   ([y2] + ebias + free) if t == 0 else ())
                p = PE(lambda e, t=t, b=b: e.matmul(psum[:, b, P * t:P * (t + 1)], YT[:, c, P * t:P * (t + 1)], woutT[:], start=False, stop=True))
            yield
            m = DVE(lambda e, b=b: e.tensor_tensor(X[:, TPC * c:TPC * (c + 1), :], psum[:, b, :].rearrange("p (t d) -> p t d", t=TPC),
                                                   X[:, TPC * c:TPC * (c + 1), :], ALU.add), [p] + xw[c])
            allb.give(b, m)
            xw[c] = [m]
            yield

        def W(name, kb, ob):
            width = D if name == "w3" else HID
            lo = FW[name][0] + kb * width + ob * P
            return slice(lo, lo + P)

        mlp_readers = {k: [] for k in [(n, i) for n in ("in", "hid0", "hid1", "th") for i in range(2)] + [("g", i) for i in range(4)]}
        mlp_count = [0]

        def products(jobs, after):
            def arms(e, last):
                def all_jobs(dt):
                    for b, high, low, weights in jobs:
                        n = len(weights)
                        for i, (act, w) in enumerate([(x, k) for k in range(n) for x in (high[k], low[k])]):
                            act, wt = (act, fw[:, weights[w]]) if dt is None else (act.bitcast(dt), fw[:, weights[w]].bitcast(dt))
                            m = e.matmul(psum[:, b, :], wt, act, start=i == 0, stop=i == 2 * n - 1)
                    last(m)

                with e.If_eq(low_flag[0], zero[0]):
                    all_jobs(None)
                with e.Else():
                    all_jobs(F32)

            return put("tensor", arms, after, arms=True)

        def mlp(c, ring, enter, late, store=None):
            q = c % 2

            def keep(dst, ob, value, m, engine):
                hi = SC(lambda e: e.activation(hidH[:, dst, q, ob, :], value, ACT.Copy), [m] + late + (mlp_readers[(f"hid{dst}", q)] if ob == 0 else []))
                return put(engine, lambda e: e.tensor_tensor(hidL[:, dst, q, ob, :], value, hidH[:, dst, q, ob, :].bitcast(F32), ALU.subtract), [hi])

            m = yield from norm(lambda t: X[:, TPC * c + t, :], xw[c], c)
            b, p = turn(c, m, ring)
            hi = SC(lambda e, b=b: e.activation(inH[:, q, :], psum[:, b, :], ACT.Copy), [p] + mlp_readers[("in", q)] + enter)
            ready = DVE(lambda e, b=b: e.tensor_tensor(inL[:, q, :], psum[:, b, :], inH[:, q, :].bitcast(F32), ALU.subtract), [hi])
            ring.give(b, ready)
            yield
            made, parts_of = [], []
            for ob in range(HB):
                b1, free1 = ring.take()
                b2, free2 = ring.take()
                p = products([(b1, [inH[:, q, :]], [inL[:, q, :]], [W("w1", 0, ob)]),
                              (b2, [inH[:, q, :]], [inL[:, q, :]], [W("w2", 0, ob)])], free1 + free2 + [ready, fw_in.mark])
                gk = mlp_count[0] % 4
                mlp_count[0] += 1
                m = SC(lambda e, b=b1, ob=ob: e.activation(fth[:, ob % 2, :], psum[:, b, :], ACT.Tanh, scale=glu_s[:, 0, ob:ob + 1]), [p] + mlp_readers[("th", ob % 2)] + enter)
                a = DVE(lambda e, b=b1, ob=ob: e.scalar_tensor_tensor(fth[:, ob % 2, :], fth[:, ob % 2, :], 1.0, psum[:, b, :], ALU.add, ALU.mult), [m])
                ring.give(b1, a)
                h = DVE(lambda e, b=b2, ob=ob, gk=gk: e.scalar_tensor_tensor(fg[:, gk, :], fth[:, ob % 2, :], glu_s[:, 1, ob:ob + 1], psum[:, b, :], ALU.mult, ALU.mult),
                        [a, p] + mlp_readers[("g", gk)])
                ring.give(b2, h)
                mlp_readers[("th", ob % 2)] = [h]
                for part in made + ([(ob, gk, h)] if ob == HB - 1 else []):
                    m = keep(0, part[0], fg[:, part[1], :], part[2], "gpsimd" if part[0] < HB - 1 else "vector")
                    mlp_readers[("g", part[1])] = [m]
                    parts_of.append(m)
                made = [(ob, gk, h)]
                yield
            mlp_readers[("in", q)] = [p]
            for name, src in (("h1", 0), ("h2", 1)):
                ready = parts_of[-2:] if src == 0 else [m]
                for ob in range(HB):
                    b, free = ring.take()
                    p = products([(b, [hidH[:, src, q, kb, :] for kb in range(HB)], [hidL[:, src, q, kb, :] for kb in range(HB)],
                                   [W(name, kb, ob) for kb in range(HB)])], free + ready)
                    gk = mlp_count[0] % 4
                    mlp_count[0] += 1
                    g = SC(lambda e, gk=gk, b=b, ob=ob, name=name: e.activation(fg[:, gk, :], psum[:, b, :], ACT.Gelu, scale=col(name + "_s", ob)),
                           [p] + mlp_readers[("g", gk)])
                    ring.give(b, g)
                    m = keep(1 - src, ob, fg[:, gk, :], g, "vector")
                    mlp_readers[("g", gk)] = [m]
                    yield
                mlp_readers[(f"hid{src}", q)] = [p]
            b, free = ring.take()
            p = products([(b, [hidH[:, 0, q, kb, :] for kb in range(HB)], [hidL[:, 0, q, kb, :] for kb in range(HB)],
                           [W("w3", kb, 0) for kb in range(HB)])], free + [m])
            mlp_readers[("hid0", q)] = [p]
            gk = mlp_count[0] % 4
            mlp_count[0] += 1
            y = SC(lambda e, b=b, gk=gk: e.activation(fg[:, gk, :], psum[:, b, :], ACT.Copy, scale=ws3[:, 0:1]), [p] + mlp_readers[("g", gk)])
            ring.give(b, y)
            yield
            b, free = ring.take()
            for t in range(TPC):
                p = PE(lambda e, b=b, t=t, gk=gk: e.transpose(psum[:, b, P * t:P * (t + 1)], fg[:, gk, P * t:P * (t + 1)], ident[:]),
                       ([y] + free) if t == 0 else ())
            mlp_readers[("g", gk)] = [p]
            m = DVE(lambda e, b=b: e.tensor_tensor(X[:, TPC * c:TPC * (c + 1), :], psum[:, b, :].rearrange("p (t d) -> p t d", t=TPC),
                                                   X[:, TPC * c:TPC * (c + 1), :], ALU.add), [p] + xw[c])
            ring.give(b, m)
            xw[c] = [m]
            if store:
                store(c, m)
            yield

        MLP_IN = 5

        def mlps(gens, beside, per_step):
            def steps(c, n):
                for _ in range(n):
                    next(gens[c], None)
                    if c >= NC - 2:
                        for _ in range(per_step):
                            next(beside, None)

            def pair(cs, stages):
                for n in stages:
                    for c in cs:
                        steps(c, n)

            for first in range(0, NC, 2):
                cs = (first, first + 1)
                pair(cs, [HB] * 2)
                ahead = [c for _ in range(MLP_IN) for c in (first + 2, first + 3)] if first + 2 < NC else []
                for c in cs:
                    for _ in range(HB):
                        steps(c, 1)
                        if ahead:
                            next(gens[ahead.pop(0)])
                for c in ahead:
                    next(gens[c])
                pair(cs, [1, 2])
            for _ in beside:
                pass

        def attention(enter, late):
            sbanks = Banks([0, 1, 2], readers, bank_state)
            pvb = 3
            mbanks = Banks([4, 5, 6], readers, bank_state)
            side = Banks([6, 7], readers, bank_state)
            ones_v = GP(lambda e: e.memset(vaug[:], 1.0), enter)
            k_ones = {c: dmas(f"k_ones{c}") for c in range(NC)}
            ld_rope = {c: dmas(f"rope{c}") for c in range(NC)}
            k_in = {c: dmas(f"k_rows{c}") for c in range(NC)}
            q_in = {s: dmas(f"q_rows{s}") for s in range(NC * G)}
            m_in = {s: dmas(f"m_rows{s}") for s in range(NC * G)}
            k_out = {c: dmas(f"k_parts{c}") for c in range(NC)}
            q_out = {c: dmas(f"q_parts{c}") for c in range(NC)}
            part_rows = nc.dram_tensor("part_rows", [NC, 2, PARTS, P, CH], BF16, kind="Internal").ap()
            rope_r, kp_r, qp_r, rt_r = [[], []], [], [], []
            slot_r = {}
            v_done = {}
            b4 = DVE(lambda e: e.memset(psum[:, pvb, :], 0.0), readers[pvb])
            readers[pvb] = [b4]

            def load_rope(c):
                for k in range(2):
                    dma(ld_rope[c], rope[:, c % 2, k, :], dram["rope"][k, :, CH * c:CH * (c + 1)], enter + rope_r[c % 2])

            def prepare(c, work):
                i = c % 2
                free_keys = enter if c < NC // 2 else late
                dma(k_ones[c], ks[c][KR:KR + MR, :, :].rearrange("p h t -> p (h t)"), dram["ones"].broadcast_to((MR, NH * CH)), free_keys)
                m = yield from norm(lambda t: X[:, TPC * c + t, :], xw[c], c)
                b, p = turn(c, m, work)
                xt = SC(lambda e, b=b: e.activation(XT[:, c, :], psum[:, b, :], ACT.Copy), [p] + xt_readers[c])
                work.give(b, xt)
                yield
                for what in range(2):
                    parts = [qparts[:, n, :] if what == 0 else kparts[:, n, :] for n in range(PARTS)]
                    old = qp_r if what == 0 else kp_r
                    m = []
                    for k in range(2):
                        b, free = work.take()
                        p = PE(lambda e, b=b, k=k, what=what: e.matmul(psum[:, b, :], wide[:, 2 * what + k, :], XT[:, c, :], start=True, stop=True),
                               [xt, ld_att.mark] + free)
                        m.append(DVE(lambda e, b=b, k=k: e.tensor_tensor(rt[:, k, :], psum[:, b, :], rope[:, i, k, :], ALU.mult),
                                     [p, ld_rope[c].mark] + enter + rt_r))
                        work.give(b, m[-1])
                        if k == 0:
                            yield
                    if what == 1:
                        rope_r[i] = [m[-1]]
                        if c + 2 < NC:
                            load_rope(c + 2)
                    yield
                    m = GP(lambda e: e.tensor_tensor(rt[:, 0, :], rt[:, 0, :], rt[:, 1, :], ALU.add), m)
                    m = SC(lambda e, parts=parts: e.activation(parts[0], rt[:, 0, :], ACT.Copy), [m] + old)
                    m = GP(lambda e, parts=parts: e.tensor_tensor(rt[:, 0, :], rt[:, 0, :], parts[0], ALU.subtract), [m])
                    yield
                    m = SC(lambda e, parts=parts: e.activation(parts[1], rt[:, 0, :], ACT.Copy), [m])
                    m = GP(lambda e, parts=parts: e.tensor_tensor(parts[2], rt[:, 0, :], parts[1], ALU.subtract), [m])
                    rt_r[:] = [m]
                    if what == 1:
                        dma(k_out[c], part_rows[c, 1].rearrange("n p t -> p n t"), kparts[:], [m])
                        for r, (_, n) in enumerate(PAIRS):
                            dma(k_in[c], ks[c][DK * r:DK * (r + 1), :, :],
                                part_rows[c, 1, n].rearrange("(h d) t -> d h t", d=DK), [k_out[c].mark])
                        kp_r[:] = [k_out[c].mark]
                    else:
                        dma(q_out[c], part_rows[c, 0].rearrange("n p t -> p n t"), qparts[:], [m])
                        qp_r[:] = [q_out[c].mark]
                    yield
                b, free = work.take()
                for t in range(TPC):
                    p = PE(lambda e, b=b, t=t: e.matmul(psum[:, b, P * t:P * (t + 1)], XT[:, c, P * t:P * (t + 1)], wide[:, 4, :], start=True, stop=True),
                           free if t == 0 else ())
                xt_readers[c] = [p]
                v = SC(lambda e, b=b: e.activation(vaug[:, TPC * c:TPC * (c + 1), :, 0:DK],
                                                   psum[:, b, :].rearrange("p (t h d) -> p t h d", t=TPC, h=NH), ACT.Copy), [p, ones_v])
                work.give(b, v)
                v_done[c] = v
                yield

            def load_q(s):
                c, g = divmod(s, NH // G)
                for r, (n, _) in enumerate(PAIRS):
                    dma(q_in[s], qs[s % QS][DK * r:DK * (r + 1), :, :],
                        part_rows[c, 0, n, G * DK * g:G * DK * (g + 1)].rearrange("(h d) t -> d h t", d=DK),
                        [q_out[c].mark] + (enter if s % QS < QS // 2 else late) + slot_r.get(s % QS, []))

            all_max = {}
            n_steps = NC * (NH // G)

            def max_units(s):
                c, g = divmod(s, NH // G)
                i = s % 2
                for hh in range(G):
                    h = G * g + hh
                    for t in range(TPC):
                        keys = P * (TPC * c + t + 1)
                        for k in range(c + 1):
                            n = min(CH, keys - CH * k)
                            diag = k == c
                            b, free = mbanks.take()
                            p = PE(lambda e, b=b, t=t, k=k, n=n, hh=hh, h=h, diag=diag:
                                   e.matmul(psum[:, b, 0:n], qs[s % QS][0:KR, hh, P * t:P * (t + 1)], ks[k][0:KR, h, 0:n],
                                            start=True, stop=not diag), free + [q_in[s].mark, k_in[k].mark])
                            if diag:
                                p = PE(lambda e, b=b, n=n: e.matmul(psum[:, b, n - P:n], identb[:], mask_qk[:], start=False, stop=True))
                            m = DVE(lambda e, b=b, n=n, hh=hh, t=t, k=k: e.tensor_reduce(mpart[:, i, hh, t, k:k + 1], psum[:, b, 0:n], AX.X, ALU.max), [p] + enter)
                            mbanks.give(b, m)
                            yield
                all_max[s] = m

            def max_stream():
                rows_of = iter(())
                for s in range(n_steps):
                    for n, _ in enumerate(max_units(s)):
                        yield
                        if n in (1, 4):
                            next(rows_of, None)
                    rows_of = max_rows(s)
                    next(rows_of)
                for _ in rows_of:
                    pass

            n_max = [G * TPC * (s // (NH // G) + 1) for s in range(n_steps)]
            stream, taken = max_stream(), [0]

            def maxima_up_to(at):
                s, part = int(at), at - int(at)
                ahead = lambda s: sum(n_max[:s + 1]) + (LEAD * n_max[s + 1] if s + 1 < n_steps else LEAD * n_max[-1])
                target = ahead(s) if part == 0 else (1 - part) * ahead(s) + part * ahead(s + 1)
                while taken[0] < target and next(stream, "end") != "end":
                    taken[0] += 1

            def max_rows(s):
                i, m = s % 2, all_max[s]
                c = s // (NH // G)
                m = DVE(lambda e: e.tensor_reduce(mall[:, i, :, :].rearrange("p t h -> p h t"), mpart[:, i, :, :, 0:c + 1], AX.X, ALU.max, negate=True), [m])
                m = DVE(lambda e: e.tensor_copy(mneg[:, i, :, 0, :], mall[:, i, :, :]), [m])
                m = DVE(lambda e: e.tensor_tensor(mneg[:, i, :, 1, :], mall[:, i, :, :], mneg[:, i, :, 0, :], ALU.subtract), [m])
                yield
                b, free = side.take()
                pt = psum[:, b, :].bitcast(BF16)
                for t in range(TPC):
                    p = PE(lambda e, t=t: e.transpose(pt[0:MR * G, P * t:P * (t + 1)], mneg[:, i, t, :, :].rearrange("p m h -> p (m h)"), identb[:]),
                           ([m] + free) if t == 0 else ())
                m = DVE(lambda e: e.tensor_copy(mrow[:, i, :], pt[0:MR * G, 0:CH]), [p] + ([m_in[s - 2].mark] if s >= 2 else []))
                side.give(b, m)
                for r in range(MR):
                    dma(m_in[s], qs[s % QS][KR + r:KR + r + 1, :, :], mrow[G * r:G * (r + 1), i, :], [m], engine="gpsimd")
                yield

            def exact(s, side_work, tail):
                c, g = divmod(s, NH // G)
                n_tiles = TPC * (c + 1)
                exps, used = {}, {}

                def scores(k, hh):
                    lo = max(0, k - TPC * c) * P
                    h = G * g + hh
                    b, free = sbanks.take()
                    diag = k >= TPC * c
                    p = PE(lambda e, b=b: e.matmul(psum[:, b, lo:CH], ks[k // TPC][:, h, P * (k % TPC):P * (k % TPC + 1)], qs[s % QS][:, hh, lo:CH], start=True, stop=not diag),
                           free + [m_in[s].mark, k_in[k // TPC].mark, k_ones[k // TPC].mark])
                    if diag:
                        p = PE(lambda e, b=b: e.matmul(psum[:, b, lo:lo + P], identb[:], mask_kq[:], start=False, stop=True))
                    i = pr_count[0] % PR
                    pr_count[0] += 1
                    used[(k, hh)] = i
                    x = SC(lambda e, b=b: e.activation(prob[:, i, lo:CH], psum[:, b, lo:CH], ACT.Exp, scale=SCALE), [p] + late + prob_r[i])
                    sbanks.give(b, x)
                    exps[k] = x

                def values(k):
                    lo = max(0, k - TPC * c) * P
                    first, end = k == 0, k == n_tiles - 1
                    for hh in range(G):
                        h, i = G * g + hh, used[(k, hh)]
                        p = PE(lambda e, h=h, hh=hh, i=i: e.matmul(psum[32 * hh:32 * hh + DK + 1, pvb, lo:CH], vaug[:, k, h, :], prob[:, i, lo:CH],
                                                                   start=first, stop=end, skip_group_check=True),
                               [exps[k]] + (readers[pvb] if first else []) + [v_done[k // TPC]])
                    for hh in range(G):
                        prob_r[used[(k, hh)]] = [p]
                    return p

                for k in range(n_tiles):
                    for hh in range(G):
                        if hh == 2 and k > 0:
                            pv = values(k - 1)
                        scores(k, hh)
                        maxima_up_to(s + (k * G + hh + 1) / (G * n_tiles))
                    side_work()
                    if k > 0:
                        next(tail, None)
                pv = values(n_tiles - 1)
                for _ in tail:
                    pass
                slot_r[s % QS] = [pv]
                ev = DVE(lambda e: e.tensor_copy(cu[:], psum[:, pvb, :]), [pv] + cu_r)
                readers[pvb] = [ev]

                def finish():
                    b, free = side.take()
                    for t in range(TPC):
                        p = PE(lambda e, t=t, b=b: e.transpose(psum[:, b, P * t:P * (t + 1)], cu[:, P * t:P * (t + 1)], ident[:]), ([ev] + free) if t == 0 else ())
                    cu_r[:] = [p]
                    view = psum[:, b, :].rearrange("p (t h r) -> p t h r", t=TPC, h=G)
                    m = DVE(lambda e: e.reciprocal(rl[:], view[:, :, :, DK]), [p])
                    m = DVE(lambda e: e.tensor_tensor(cx[:, :, G * g * DK:G * (g + 1) * DK].rearrange("p t (h d) -> p t h d", h=G), view[:, :, :, 0:DK],
                                                      rl[:].unsqueeze(3).broadcast_to((P, TPC, G, DK)), ALU.mult), [m] + (cx_r if g == 0 else []))
                    side.give(b, m)
                    yield
                    if g < NH // G - 1:
                        return
                    b, free = side.take()
                    for t in range(TPC):
                        p = PE(lambda e, t=t, b=b: e.transpose(psum[:, b, P * t:P * (t + 1)], cx[:, t, :], ident[:]), ([m] + free) if t == 0 else ())
                    cx_r[:] = [p]
                    m = SC(lambda e, b=b: e.activation(cxT[:], psum[:, b, :], ACT.Copy), [p] + cxt_r)
                    side.give(b, m)
                    yield
                    b, free = side.take()
                    for t in range(TPC):
                        p = PE(lambda e, t=t, b=b: e.matmul(psum[:, b, P * t:P * (t + 1)], cxT[:, P * t:P * (t + 1)], wo[:], start=True, stop=True),
                               ([m] + free) if t == 0 else ())
                    cxt_r[:] = [p]
                    m = DVE(lambda e, b=b: e.tensor_tensor(X[:, TPC * c:TPC * (c + 1), :], psum[:, b, :].rearrange("p (t d) -> p t d", t=TPC),
                                                           X[:, TPC * c:TPC * (c + 1), :], ALU.add), [p] + xw[c])
                    side.give(b, m)
                    xw[c] = [m]

                return finish()

            prob_r = [[] for _ in range(PR)]
            pr_count = [0]
            cu_r, cx_r, cxt_r = [], [], []

            def begin():
                for c in range(2):
                    load_rope(c)
                first, second = prepare(0, allb), prepare(1, allb)
                for _ in range(5):
                    for one in (first, second):
                        next(one)
                        yield
                yield from first
                load_q(0)
                load_q(1)
                yield from second
                for n in range(int(n_max[0] + LEAD * n_max[1])):
                    next(stream)
                    taken[0] += 1
                    yield

            def run(beside):
                tail = iter(())
                for s in range(n_steps):
                    c, g = divmod(s, NH // G)
                    if g == 0:
                        jobs = prepare(c + 2, side) if c + 2 < NC else iter(())
                    if s == n_steps - 2:
                        jobs = beside

                    def side_work(jobs=jobs):
                        next(jobs, None)

                    if s + 2 < n_steps:
                        if g == NH // G - 1:
                            for _ in jobs:
                                pass
                        load_q(s + 2)
                    tail = exact(s, side_work, tail)
                for _ in tail:
                    pass

            return begin, run

        low_flag, zero = [None], [None]
        params, flagged = {}, [None]
        ebias = []

        def scales_of_mlps():
            m = DVE(lambda e: e.tensor_scalar(glu_s[:, 0, :], cols[:, COL["w1_s"][0]:COL["w1_s"][0] + HB], 0.5, None, ALU.mult), [ld_cols.mark])
            m = DVE(lambda e: e.tensor_tensor(glu_s[:, 1, :], glu_s[:, 0, :], cols[:, COL["w2_s"][0]:COL["w2_s"][0] + HB], ALU.mult), [m])
            return DVE(lambda e: e.tensor_scalar(ws3[:], col("w3_s"), 0.5, None, ALU.mult), [ld_cols.mark])

        wave([(LAG * c, in_turn(moe(c, ebias), ssm_front(c))) for c in range(NC)] + [(1, split_bias()), (2 * LAG, ssm_params(params))])
        wave([(0, ssm_conv(params)), (0, check_mlp_weights())])
        entered, late = [], []
        gens = {c: mlp(c, allb, entered, late) for c in range(NC)}

        def mlp_norm(c):
            for _ in range(MLP_IN - 1 if c < 2 else 0):
                next(gens[c])
                yield

        wave([(LAG * c, in_turn(ssm_tail(c, ebias), moe(c, ebias), mlp_norm(c))) for c in range(NC)])
        scales = scales_of_mlps()

        def read_flag(e):
            low_flag[0] = e.alloc_register("low_part_flag")
            e.reg_load(low_flag[0], flag[0:1, 0:1])
            zero[0] = e.alloc_register("no_low")
            e.reg_mov(zero[0], 0)

        def barrier():
            return [next(m for f, _, m, _ in reversed(queues[n]) if m is not None and f is not read_flag)
                    for n in ("tensor", "vector", "scalar", "gpsimd")]

        PE(read_flag, [flagged[0]])
        y_out = dmas("y_out")
        yv = out.rearrange("b (j p) d -> p (b j) d", p=P)

        def store(c, m):
            dma(y_out, yv[:, TPC * c:TPC * (c + 1), :], X[:, TPC * c:TPC * (c + 1), :], [m])

        def inputs(gens, n=MLP_IN):
            for _ in range(n):
                for c in (0, 1):
                    next(gens[c])
                    yield

        entered[:] = barrier() + [scales]
        late[:] = entered
        begin, run = attention(entered, late)
        for _ in inputs(gens, 1):
            pass
        mlps(gens, begin(), 2)
        late[:] = barrier()
        ring = Banks([7], readers, bank_state)
        hidden_free = []
        gens = {c: mlp(c, ring if c < 2 else allb, [], hidden_free, store) for c in range(NC)}
        run(inputs(gens))
        ring.ids = allb.ids
        hidden_free[:] = barrier()
        mlps(gens, iter(()), 0)

        for n in sems:
            k = 0
            for _, _, m, _ in queues[n]:
                if m is not None and m.used:
                    k += 1
                    m.value = k

        block = ctx.enter_context(nc.Block())

        def emit(name, e):
            seen = {}
            for fn, after, m, group in queues[name]:
                for a in after:
                    if isinstance(a.owner, Dmas):
                        key, sem, value = id(a.owner), a.owner.sem, 16 * a.owner.n
                    else:
                        key, sem, value = a.owner, sems[a.owner], a.value
                    if seen.get(key, 0) < value:
                        e.wait_ge(sem, value)
                        seen[key] = value
                if group == "arms":
                    fn(e, (lambda i: i.then_inc(sems[name], 1)) if m.used else (lambda i: i))
                    continue
                i = fn(e)
                if group is not None:
                    i.then_inc(group.sem, 16)
                elif m.used:
                    i.then_inc(sems[name], 1)

        @block.sync
        def _(e):
            emit("sync", e)
            e.wait_ge(y_out.sem, 16 * y_out.n)

        @block.gpsimd
        def _(e):
            emit("gpsimd", e)

        @block.scalar
        def _(e):
            emit("scalar", e)

        @block.vector
        def _(e):
            emit("vector", e)

        @block.tensor
        def _(e):
            emit("tensor", e)


def kernel(**inputs):
    import ml_dtypes
    import concourse.bacc as bacc
    from concourse.bass_utils import run_bass_kernel_spmd as run

    a = {k: np.asarray(v) for k, v in inputs.items()}
    c = np.ascontiguousarray
    arrays = {}
    arrays["x"] = c(a["L0_attn_x"].reshape(T, D))
    arrays["ident"] = np.eye(P, dtype=np.float32)
    sel = np.zeros((P, P))
    sel[list(BIAS_ROWS)] = 1
    arrays["partsel"] = sel.astype(ml_dtypes.bfloat16)
    arrays["mirror"] = c(np.eye(P, dtype=np.float32)[::-1])
    arrays["identb"] = np.eye(P).astype(ml_dtypes.bfloat16)
    upper = np.triu(np.ones((P, P)), 1) * NEG
    arrays["mask_qk"] = upper.astype(ml_dtypes.bfloat16)
    arrays["mask_kq"] = c(upper.T).astype(ml_dtypes.bfloat16)
    arrays["revidx"] = np.tile(np.arange(E, 0, -1, dtype=np.float32), TPC)[None]
    arrays["steps"] = np.arange(P, -1, -1, dtype=np.float32)[None]
    arrays["back"] = np.arange(P - 1, -1, -1, dtype=np.float32)[:, None]
    arrays["ones"] = np.ones((1, NH * CH), ml_dtypes.bfloat16)
    arrays["router_w"] = a["L0_ffn_router_w"]
    arrays["expert_wT"] = c(a["L0_ffn_expert_w"].transpose(1, 0, 2).reshape(D, E * D))
    vec = lambda v: v.reshape(-1, P).T
    arrays["cols"] = c(np.concatenate([
        vec(a["L0_attn_ln_g"]), vec(a["L0_attn_ln_b"]), vec(a["L0_attn_b_in"]), vec(a["L0_attn_D_skip"]), vec(a["L0_attn_log_dt"]),
        vec(a["L1_ffn_w1_s"]), vec(a["L1_ffn_w2_s"]), vec(a["L1_ffn_h1_s"]), vec(a["L1_ffn_h2_s"]), vec(a["L1_ffn_w3_s"]),
        a["L0_attn_A_log"]], axis=1))
    arrays["rows"] = c(np.concatenate([
        a["L0_ffn_router_b"], a["L0_ffn_expert_b"].reshape(-1), a["L0_attn_b_out"], a["L0_attn_log_dt"],
        a["L0_attn_A_log"].T.reshape(-1)])[None])
    arrays["W_inT"] = c(a["L0_attn_W_in"].T)
    arrays["W_outT"] = c(a["L0_attn_W_out"].T)
    arrays["W_BT"] = c(a["L0_attn_W_B"].T)
    arrays["W_CT"] = c(a["L0_attn_W_C"].T)
    swap = np.arange(D) ^ 1
    wq, wk = a["L1_attn_Wq"], a["L1_attn_Wk"]
    arrays["wide"] = c(np.stack([wq.T, wq[swap].T, wk.T, wk[swap].T, a["L1_attn_Wv"].T]))
    arrays["WoT"] = c(a["L1_attn_Wo"].T)
    blocks = lambda w: w.T.reshape(-1, P, w.shape[0]).transpose(1, 0, 2).reshape(P, -1)
    arrays["mlp_w"] = c(np.concatenate([blocks(a[f"L1_ffn_{n}_w"]) for n in ("w1", "w2", "h1", "h2", "w3")], axis=1))
    freq = (np.float32(1.0) / np.float32(10000.0) ** (np.arange(0, DK, 2, dtype=np.float32) / np.float32(DK))).astype(np.float32)
    angle = (np.arange(T, dtype=np.float32)[None, :] * freq[:, None]).astype(np.float32)
    cos, sin = np.cos(angle).astype(np.float32), np.sin(angle).astype(np.float32)
    cos8, sin8 = np.repeat(cos, 2, axis=0), np.stack([-sin, sin], axis=1).reshape(DK, T)
    arrays["rope"] = c(np.stack([np.tile(cos8, (NH, 1)), np.tile(sin8, (NH, 1))]))

    nc = bacc.Bacc("TRN2", target_bir_lowering=False, num_devices=1)
    dram, fed = {}, {}
    for name, v in arrays.items():
        fed[f"in_{name}"] = v
        dram[name] = nc.dram_tensor(f"in_{name}", v.shape, mybir.dt.from_np(v.dtype), kind="ExternalInput").ap()
    out = nc.dram_tensor("out", (1, T, D), F32, kind="ExternalOutput").ap()
    build(nc, dram, out)
    r = run(nc, [fed], core_ids=[0])
    return r.results[0]["out"]
```
